# Optimizing a Trainium2 kernel written in Bass

```python
import numpy as np
import jax
import jax.numpy as jnp

def _softmax(x, axis=-1):
    return jax.nn.softmax(x, axis=axis)

def _gelu(x):
    return jax.nn.gelu(x, approximate=True)

def _silu(x):
    return jax.nn.silu(x)

def _sigmoid(x):
    return jax.nn.sigmoid(x)

def _layernorm(x, axis=-1, eps=1e-05):
    m = jnp.mean(x, axis=axis, keepdims=True)
    v = jnp.var(x, axis=axis, keepdims=True)
    return (x - m) / jnp.sqrt(v + eps)

def _scatter_add(tgt, idx, src, axis=0):
    return tgt.at[idx].add(src)

def _segment_sum(src, seg, n):
    return jax.ops.segment_sum(src, seg, n)
kernel_name = 'mk_flamingo_gated_d1_seqx_r8_45351f'

def setup_inputs(seed: int=0):
    np.random.seed(seed)
    _w = jnp.asarray

    def _rec_inputs():
        import jax
        import jax.numpy as jnp
        _rk = jax.random.key(seed)
        x = 0.000341 + 1 * jax.random.normal(jax.random.fold_in(_rk, 1), (8, 128, 256), jnp.float32)
        _lenS = 128 - jax.random.randint(jax.random.fold_in(_rk, 7), (8,), 0, max(1, 128 // 4) + 1, jnp.int32)
        _lenS2 = 128 - jax.random.randint(jax.random.fold_in(_rk, 8), (8,), 0, max(1, 128 // 4) + 1, jnp.int32)
        _ctx_2048P = jax.random.normal(jax.random.fold_in(_rk, 11), (8, 16, 256), jnp.float32)
        _ctx_2048c = jax.random.dirichlet(jax.random.fold_in(_rk, 511), 0.3 * jnp.ones((16,), jnp.float32), (8, 128))
        _ctx_2048t = jnp.einsum('bsk,bkd->bsd', _ctx_2048c, _ctx_2048P)
        _ctx_2048t = _ctx_2048t * jax.lax.rsqrt(jnp.mean(jnp.square(_ctx_2048t)) + 1e-12) * 0.953939
        ctx_2048 = -1.47943e-05 + 1.00017 * (_ctx_2048t + 0.3 * jax.random.normal(jax.random.fold_in(_rk, 611), (8, 128, 256), jnp.float32))
        _g = jax.random.normal(jax.random.fold_in(_rk, 9001), (2, 1), jnp.float32)
        _g = jnp.sign(_g) * jnp.maximum(jnp.abs(_g), 1.0) + (_g == 0) * 1.0
        g_xattn = _g[0]
        g_ffn = _g[1]
        return (x, ctx_2048, g_xattn, g_ffn)
    x, ctx_2048, g_xattn, g_ffn = _rec_inputs()

    def _L0_xattn_setup():
        import jax, jax.numpy as jnp
        import numpy as np

        def _wkv(time_decay, time_first, k, v):
            w = -jnp.exp(time_decay)
            u = time_first
            B, T, C = k.shape
            aa = jnp.zeros((B, C), dtype=k.dtype)
            bb = jnp.zeros((B, C), dtype=k.dtype)
            pp = jnp.full((B, C), -1e+38, dtype=k.dtype)

            def step(carry, kv_t):
                aa, bb, pp = carry
                kt, vt = kv_t
                ww = u + kt
                q = jnp.maximum(pp, ww)
                e1 = jnp.exp(pp - q)
                e2 = jnp.exp(ww - q)
                y_t = (e1 * aa + e2 * vt) / (e1 * bb + e2)
                ww2 = pp + w
                q2 = jnp.maximum(ww2, kt)
                e1b = jnp.exp(ww2 - q2)
                e2b = jnp.exp(kt - q2)
                new_carry = (e1b * aa + e2b * vt, e1b * bb + e2b, q2)
                return (new_carry, y_t)
            ks = jnp.transpose(k, (1, 0, 2))
            vs = jnp.transpose(v, (1, 0, 2))
            _, ys = jax.lax.scan(step, (aa, bb, pp), (ks, vs))
            return jnp.transpose(ys, (1, 0, 2))
        key = jax.random.key(seed)
        k1, k2, k3, k4 = jax.random.split(key, 4)
        B, T, C = (8, 128, 256)
        return {'batch_size': B, 'seq_len': T, 'embedding_dim': C, 'time_decay': jax.random.normal(k1, (C,), dtype=jnp.float32), 'time_first': jax.random.normal(k2, (C,), dtype=jnp.float32), 'k': jax.random.normal(k3, (B, T, C), dtype=jnp.float32), 'v': jax.random.normal(k4, (B, T, C), dtype=jnp.float32)}
    _L0_xattn_all = _L0_xattn_setup()
    _L0_xattn_in = {k: v for k, v in _L0_xattn_all.items() if k in ('time_decay', 'time_first')}
    del _L0_xattn_all

    def _L0_ffn_setup():
        import jax, jax.numpy as jnp
        import numpy as np
        H = 256
        I = 176
        E = 16
        K = 2
        SI = I * 2

        def _swiglu(gu, inter):
            g, u = (gu[..., :inter], gu[..., inter:])
            return jax.nn.silu(g) * u
        key = jax.random.key(seed)
        ks = jax.random.split(key, 6)
        s = 0.02
        hidden_states = jax.random.normal(ks[0], (1, 128, H), dtype=jnp.float32)
        gate_w = jax.random.normal(ks[1], (E, H), dtype=jnp.float32) * s
        w_gate_up = jax.random.normal(ks[2], (E, H, 2 * I), dtype=jnp.float32) * s
        w_down = jax.random.normal(ks[3], (E, I, H), dtype=jnp.float32) * s
        shared_gate_up = jax.random.normal(ks[4], (H, 2 * SI), dtype=jnp.float32) * s
        shared_down = jax.random.normal(ks[5], (SI, H), dtype=jnp.float32) * s
        return {'hidden_states': hidden_states, 'gate_w': gate_w, 'w_gate_up': w_gate_up, 'w_down': w_down, 'shared_gate_up': shared_gate_up, 'shared_down': shared_down}
    _L0_ffn_all = _L0_ffn_setup()
    _L0_ffn_in = {k: v for k, v in _L0_ffn_all.items() if k in ('gate_w', 'w_gate_up', 'w_down', 'shared_gate_up', 'shared_down')}
    del _L0_ffn_all
    return {'x': x, 'ctx_2048': ctx_2048, 'g_xattn': g_xattn, 'g_ffn': g_ffn, 'L0_xattn_time_decay': _L0_xattn_in['time_decay'], 'L0_xattn_time_first': _L0_xattn_in['time_first'], 'L0_ffn_gate_w': _L0_ffn_in['gate_w'], 'L0_ffn_w_gate_up': _L0_ffn_in['w_gate_up'], 'L0_ffn_w_down': _L0_ffn_in['w_down'], 'L0_ffn_shared_gate_up': _L0_ffn_in['shared_gate_up'], 'L0_ffn_shared_down': _L0_ffn_in['shared_down']}

def reference(x, ctx_2048, g_xattn, g_ffn, L0_xattn_time_decay, L0_xattn_time_first, L0_ffn_gate_w, L0_ffn_w_gate_up, L0_ffn_w_down, L0_ffn_shared_gate_up, L0_ffn_shared_down):
    import jax
    import jax.numpy as jnp

    def _L0_xattn_ref(batch_size, seq_len, embedding_dim, time_decay, time_first, k, v):
        import jax, jax.numpy as jnp
        import numpy as np

        def _wkv(time_decay, time_first, k, v):
            w = -jnp.exp(time_decay)
            u = time_first
            B, T, C = k.shape
            aa = jnp.zeros((B, C), dtype=k.dtype)
            bb = jnp.zeros((B, C), dtype=k.dtype)
            pp = jnp.full((B, C), -1e+38, dtype=k.dtype)

            def step(carry, kv_t):
                aa, bb, pp = carry
                kt, vt = kv_t
                ww = u + kt
                q = jnp.maximum(pp, ww)
                e1 = jnp.exp(pp - q)
                e2 = jnp.exp(ww - q)
                y_t = (e1 * aa + e2 * vt) / (e1 * bb + e2)
                ww2 = pp + w
                q2 = jnp.maximum(ww2, kt)
                e1b = jnp.exp(ww2 - q2)
                e2b = jnp.exp(kt - q2)
                new_carry = (e1b * aa + e2b * vt, e1b * bb + e2b, q2)
                return (new_carry, y_t)
            ks = jnp.transpose(k, (1, 0, 2))
            vs = jnp.transpose(v, (1, 0, 2))
            _, ys = jax.lax.scan(step, (aa, bb, pp), (ks, vs))
            return jnp.transpose(ys, (1, 0, 2))
        assert seq_len <= 128
        return _wkv(time_decay, time_first, k, v)

    def _L0_ffn_ref(hidden_states, gate_w, w_gate_up, w_down, shared_gate_up, shared_down):
        import jax, jax.numpy as jnp
        import numpy as np
        H = 256
        I = 176
        E = 16
        K = 2
        SI = I * 2

        def _swiglu(gu, inter):
            g, u = (gu[..., :inter], gu[..., inter:])
            return jax.nn.silu(g) * u
        orig_shape = hidden_states.shape
        x = hidden_states.reshape(-1, H)
        logits = jnp.einsum('th,eh->te', x, gate_w)
        scores = jax.nn.softmax(logits, axis=-1)
        topk_w, topk_idx = jax.lax.top_k(scores, K)
        combine = jnp.sum(jax.nn.one_hot(topk_idx, E, dtype=x.dtype) * topk_w[..., None], axis=1)
        gu = jnp.einsum('th,ehj->etj', x, w_gate_up)
        h = _swiglu(gu, I)
        y = jnp.einsum('eti,eih,te->th', h, w_down, combine)
        gu_s = x @ shared_gate_up
        y = y + _swiglu(gu_s, SI) @ shared_down
        return y.reshape(orig_shape)
    x = x + jnp.tanh(g_xattn[0]) * _L0_xattn_ref(8, 128, 256, L0_xattn_time_decay, L0_xattn_time_first, _layernorm(x, axis=-1), ctx_2048)
    x = x + jnp.tanh(g_ffn[0]) * _L0_ffn_ref(_layernorm(x, axis=-1), L0_ffn_gate_w, L0_ffn_w_gate_up, L0_ffn_w_down, L0_ffn_shared_gate_up, L0_ffn_shared_down)
    return x

_drawn_inputs = setup_inputs


def setup_inputs(seed=0):
    import zlib

    import numpy as np

    out = dict(_drawn_inputs(seed))
    spreads = {}
    factors = {'L0_ffn_gate_w': 8.0,
     'L0_ffn_w_gate_up': 8.0,
     'L0_ffn_w_down': 8.0,
     'L0_ffn_shared_gate_up': 3.482,
     'L0_ffn_shared_down': 3.47}
    for name, (base, spread) in spreads.items():
        noise = np.random.default_rng([zlib.crc32(name.encode()), seed]).standard_normal(out[name].shape)
        drawn = base * np.exp(spread * noise) if base else spread * noise
        out[name] = jnp.asarray(drawn.astype(out[name].dtype))
    for name, factor in factors.items():
        out[name] = (out[name] * factor).astype(out[name].dtype)
    return out
```

```python
from contextlib import ExitStack

import concourse.bass as bass
from concourse import mybir

ALU = mybir.AluOpType
ACT = mybir.ActivationFunctionType
AX = mybir.AxisListType
F32 = mybir.dt.float32
F16 = mybir.dt.float16
BF16 = mybir.dt.bfloat16
U32 = mybir.dt.uint32
I32 = mybir.dt.int32

P = 128
EPS = 1e-5
NEG = -1e38


def gated_wkv_moe(nc, x, ctx_in, g_xattn, g_ffn, decay, first, gate_w, w_gate_up, w_down, s_gate_up, s_down, out):
    NB, T, D = x.shape
    NE, _, J2 = w_gate_up.shape
    J = J2 // 2
    S2 = s_gate_up.shape[1]
    SJ = S2 // 2
    NTOK = NB * T
    DC = D // P
    JH = J // 2
    PAIRS = 2 * NTOK
    NT = PAIRS // P + NE - 1
    NTP = 32
    SEQ = 2 * DC
    TP = T + 1
    NCH = NB // 2
    SCH = [(k * P, min(P, SJ - k * P)) for k in range((SJ + P - 1) // P)]
    assert T == P and DC == 2 and NT < NTP and JH <= P and PAIRS <= 2048

    xn_rows = nc.dram_tensor("xn_rows", (NTOK, D), F32, kind="Internal").ap()
    y_rows = nc.dram_tensor("y_rows", (PAIRS + NT * P, D), F32, kind="Internal").ap()

    with ExitStack() as ctx:
        def sb(name, shape, dt=F32):
            return ctx.enter_context(nc.sbuf_tensor(name, shape, dt))

        def psum(name, shape, dt=F32):
            return ctx.enter_context(nc.psum_tensor(name, shape, dt))

        def sem(name):
            return ctx.enter_context(nc.semaphore(name))

        w_gu = sb("w_gu", [P, NE, DC, J2])
        w_dn = sb("w_dn", [JH, NE, 2, D])
        s_gu = sb("s_gu", [P, DC, S2])
        s_dn = sb("s_dn", [P, len(SCH), D])
        gate_rows = sb("gate_rows", [NE, D])
        gate_t = sb("gate_t", [P, DC, NE])
        x1 = sb("x1", [P, NB, D])
        xg = sb("xg", [P, NTP, D])
        kn = xg[:, 0:NB, :]
        v_rows = xg[:, NB:2 * NB, :]
        wk = xg[:, 2 * NB:NTP, :].rearrange("p n d -> p (n d)").rearrange("p (q s t) -> p q s t", s=SEQ, t=T)
        yw, e2v, num, den, diff = wk[:, 0:2], wk[:, 2:4], wk[:, 4], wk[:, 5], wk[:, 6]
        y2 = xg[:, 0:2 * NB, :].rearrange("p (b k) d -> p b k d", k=2)
        xn = sb("xn", [P, 4, D])
        stats = sb("stats", [P, NB, 6])
        mv = sb("mv", [P, NB, 2])
        vpe = sb("vpe", [P, NB])
        rstd = sb("rstd", [P, 2, NB])
        neg_half = sb("neg_half", [P, NB])
        kv = sb("kv", [P, 2, 2, SEQ, TP])
        pp = sb("pp", [P, 2, SEQ, TP])
        ex = sb("ex", [P, 2, 4, SEQ, TP])
        vb = sb("vb", [P, SEQ, TP])
        aa = sb("aa", [P, SEQ, TP])
        bb = sb("bb", [P, SEQ, TP])
        decay_t = sb("decay_t", [P, SEQ, TP])
        cols = sb("cols", [P, 2, DC])
        wcol = sb("wcol", [P, DC])
        gates = sb("gates", [P, 2])
        tg = sb("tg", [P, 2])
        xnT = sb("xnT", [P, 2, DC, P])
        th = sb("th", [P, 2, SJ])
        hs = sb("hs", [P, 2, SJ])
        hsT = sb("hsT", [P, 2, len(SCH), P])
        lg = sb("lg", [P, NB, NE])
        top = sb("top", [P, NB, 8])
        topi = sb("topi", [P, NB, 8], U32)
        mask = sb("mask", [P, 2, NB, NE], BF16)
        both = sb("both", [P, NB + 1, NE], BF16)
        over = sb("over", [P, NE, NB])
        tiles = sb("tiles", [P, NE])
        ends = sb("ends", [P, NE])
        begins = sb("begins", [P, NE])
        slot_e = sb("slot_e", [P, NB, NE])
        slot_m = sb("slot_m", [P, 2, NB, NE])
        slot = sb("slot", [P, 2 * NB])
        slot_u = sb("slot_u", [P, 2 * NB], U32)
        row_u = sb("row_u", [P, 2 * NB], U32)
        tile_u = sb("tile_u", [P, 2 * NB], U32)
        row_f = sb("row_f", [P, 2 * NB])
        row_hot = sb("row_hot", [P, 2 * NB, P], F16)
        tile_hot = sb("tile_hot", [P, 2 * NB, NTP], F16)
        tile_val = sb("tile_val", [P, 2 * NB, NTP], F16)
        pad_val = sb("pad_val", [P, NTP])
        pair_u = sb("pair_u", [P, NTP], U32)
        token_u = sb("token_u", [P, NTP], U32)
        before = sb("before", [1, NTP, NE])
        owner_f = sb("owner_f", [1, NTP])
        owner = sb("owner", [1, NTP], I32)
        esub = sb("esub", [P, NB, NE])
        etop = sb("etop", [P, NB])
        esum = sb("esum", [P, NB])
        wts = sb("wts", [P, 2, NB])
        xgT = sb("xgT", [P, 2, DC, P])
        sg = sb("sg", [P, 2, J])
        h = sb("h", [P, 2, J])
        hT = sb("hT", [JH, 2, 2, P])
        yt = sb("yt", [P, 2, D])
        ident = sb("ident", [P, P])
        tri = sb("tri", [P, P], BF16)
        ones = sb("ones", [P, P], BF16)
        ones_f = sb("ones_f", [P, NE])
        iota_e = sb("iota_e", [P, NE])
        iota_t = sb("iota_t", [P, NTP])
        iota_r = sb("iota_r", [P, P], F16)
        pair_no = sb("pair_no", [P, 2 * NB], F16)
        limits = sb("limits", [P, NB])
        pad_row = sb("pad_row", [P, NTP])

        bank_in = psum("bank_in", [P, 2, 512])
        bank_y = psum("bank_y", [P, 512])
        bank_x = psum("bank_x", [P, 512])
        bank_l = psum("bank_l", [P, 512])
        bank_g = psum("bank_g", [P, 2, 512])
        bank_h = psum("bank_h", [P, 512])

        x_in = [sem(f"x_in{c}") for c in range(NCH)]
        v_in = [sem(f"v_in{c}") for c in range(NCH)]
        small_in = sem("small_in")
        shared_in = sem("shared_in")
        experts_in = sem("experts_in")
        xn_stored = [sem(f"xn_stored{q}") for q in range(4)]
        rows_gathered = [sem(f"rows_gathered{q}") for q in range(4)]
        rows_scattered = [sem(f"rows_scattered{q}") for q in range(2)]
        y_back = [sem(f"y_back{b}") for b in range(NB)]
        out_stored = sem("out_stored")
        dve_step = sem("dve_step")
        pool_step = sem("pool_step")
        act_step = sem("act_step")
        consts_ready = sem("consts_ready")
        pads_ready = sem("pads_ready")
        gates_ready = sem("gates_ready")
        decay_ready = sem("decay_ready")
        var_ready = sem("var_ready")
        rstd_ready = sem("rstd_ready")
        kn_ready = sem("kn_ready")
        in_turned = sem("in_turned")
        kv_ready = sem("kv_ready")
        args_ready = sem("args_ready")
        exps_ready = sem("exps_ready")
        e2v_ready = sem("e2v_ready")
        yw_ready = sem("yw_ready")
        yw_turned = sem("yw_turned")
        x1_ready = sem("x1_ready")
        xn_ready = sem("xn_ready")
        xn_turned = sem("xn_turned")
        xnT_ready = sem("xnT_ready")
        gate_turned = sem("gate_turned")
        gate_ready = sem("gate_ready")
        logits_ready = sem("logits_ready")
        sgu_ready = sem("sgu_ready")
        sth_ready = sem("sth_ready")
        hs_ready = sem("hs_ready")
        hs_turned = sem("hs_turned")
        hsT_ready = sem("hsT_ready")
        sy_ready = sem("sy_ready")
        sy_added = sem("sy_added")
        both_ready = sem("both_ready")
        ranks_ready = sem("ranks_ready")
        hot_ready = sem("hot_ready")
        table_ready = sem("table_ready")
        indices_ready = sem("indices_ready")
        owner_ready = sem("owner_ready")
        esub_ready = sem("esub_ready")
        eexp_ready = sem("eexp_ready")
        xg_turned = sem("xg_turned")
        xgT_ready = sem("xgT_ready")
        gu_ready = sem("gu_ready")
        sg_ready = sem("sg_ready")
        h_ready = sem("h_ready")
        h_turned = sem("h_turned")
        hT_ready = sem("hT_ready")
        y_ready = sem("y_ready")
        yt_ready = sem("yt_ready")
        out_ready = sem("out_ready")

        x_dram = x.rearrange("b t d -> t b d")
        v_dram = ctx_in.rearrange("b t d -> t b d")
        out_dram = out.rearrange("b t d -> t b d")
        xn_dram = xn_rows.rearrange("(b t) d -> t b d", t=P)
        y_dram = y_rows[0:PAIRS, :].rearrange("(k b t) d -> t b k d", t=P, k=2)
        wgu_dram = w_gate_up.rearrange("e (c p) j -> p e c j", p=P)
        wdn_dram = w_down.rearrange("e (c p) d -> p e c d", p=JH)
        t_bank = [bank_in[:, 0, :], bank_in[:, 1, :]]
        gu_bank = [bank_g[:, 0, :], bank_g[:, 1, :]]
        ht_bank = [bank_y, bank_x]
        yo_bank = [bank_l, bank_h]

        block = ctx.enter_context(nc.Block())

        @block.sync
        def _(sp):
            for c in range(NCH):
                sp.dma_start(x1[:, 2 * c:2 * c + 2, :], x_dram[:, 2 * c:2 * c + 2, :]).then_inc(x_in[c], 16)
            sp.dma_start(gate_rows[:], gate_w).then_inc(small_in, 16)
            sp.dma_start(s_gu[:], s_gate_up.rearrange("(c p) j -> p c j", p=P)).then_inc(shared_in, 16)
            for k, (at, n) in enumerate(SCH):
                sp.dma_start(s_dn[0:n, k, :], s_down[at:at + n, :]).then_inc(shared_in, 16)
            for q in range(4):
                sp.dma_start(w_gu[:, 4 * q:4 * q + 4], wgu_dram[:, 4 * q:4 * q + 4]).then_inc(experts_in, 16)
                sp.dma_start(w_dn[:, 4 * q:4 * q + 4], wdn_dram[:, 4 * q:4 * q + 4]).then_inc(experts_in, 16)
            for b in range(NB):
                sp.wait_ge(xn_ready, b + 1)
                sp.dma_start(xn_dram[:, b, :], xn[:, b % 4, :]).then_inc(xn_stored[b % 4], 16)
            sp.wait_ge(rows_scattered[0], 16 * ((NT + 1) // 2))
            sp.wait_ge(rows_scattered[1], 16 * (NT // 2))
            sp.wait_ge(xg_turned, NT)
            for b in range(NB):
                sp.dma_start(y2[:, b], y_dram[:, b]).then_inc(y_back[b], 16)
            for b in range(NB):
                sp.wait_ge(out_ready, b + 1)
                sp.dma_start(out_dram[:, b, :], x1[:, b, :]).then_inc(out_stored, 16)
            sp.wait_ge(out_stored, 16 * NB)

        @block.gpsimd
        def _(pool):
            steps = [0]

            def do(ins):
                steps[0] += 1
                ins.then_inc(pool_step, 1)

            def settle():
                pool.wait_ge(pool_step, steps[0])

            do(pool.memset(ident[:], 0.0))
            do(pool.memset(tri[:], 1.0))
            settle()
            pool.affine_select(out=ident[:], in_=ident[:], compare_op=ALU.not_equal, fill=1.0, base=0,
                               pattern=[[-1, P]], channel_multiplier=1).then_inc(consts_ready, 1)
            do(pool.memset(neg_half[:], -0.5))
            settle()

            def rsqrt(which, c):
                pool.wait_ge(var_ready, NCH * which + c + 1)
                pair = slice(2 * c, 2 * c + 2)
                pool.tensor_tensor(rstd[:, which, pair], vpe[:, pair], neg_half[:, pair],
                                   ALU.pow).then_inc(rstd_ready, 1)

            for c in range(NCH):
                rsqrt(0, c)
            pool.affine_select(out=tri[:], in_=tri[:], compare_op=ALU.is_gt, fill=0.0, base=0,
                               pattern=[[1, P]], channel_multiplier=-1).then_inc(consts_ready, 1)
            pool.memset(ones[:], 1.0).then_inc(consts_ready, 1)
            pool.memset(ones_f[:], 1.0).then_inc(consts_ready, 1)
            pool.memset(both[:, NB, :], 0.0).then_inc(consts_ready, 1)
            kw = dict(allow_small_or_imprecise_dtypes=True)
            pool.iota(iota_e[:], pattern=[[1, NE]], base=0, channel_multiplier=0, **kw).then_inc(consts_ready, 1)
            pool.iota(iota_t[:], pattern=[[1, NTP]], base=0, channel_multiplier=0, **kw).then_inc(consts_ready, 1)
            pool.iota(iota_r[:], pattern=[[1, P]], base=0, channel_multiplier=0, **kw).then_inc(consts_ready, 1)
            pool.iota(pair_no[:], pattern=[[NTOK, 2], [P, NB]], base=1, channel_multiplier=1, **kw).then_inc(consts_ready, 1)
            pool.iota(limits[:], pattern=[[P, NB]], base=0, channel_multiplier=0, **kw).then_inc(consts_ready, 1)
            pool.iota(pad_row[:], pattern=[[P, NTP]], base=PAIRS + 1, channel_multiplier=1, **kw).then_inc(consts_ready, 1)

            for c in range(NCH):
                pool.wait_ge(exps_ready, 2 * c + 2)
                if c >= 2:
                    pool.wait_ge(yw_ready, c - 1)
                pool.tensor_tensor(e2v[:, c % 2], ex[:, c % 2, 2, :, 1:TP], kv[:, c % 2, 1, :, 1:TP],
                                   ALU.mult).then_inc(e2v_ready, 1)
                rsqrt(1, c)

            def gather(i):
                pool.indirect_dma_start(xg[:, i % 4, :], None, xn_rows,
                                        bass.IndirectOffsetOnAxis(token_u[:, i:i + 1], 0)).then_inc(rows_gathered[i % 4], 16)

            def scatter(i):
                pool.wait_ge(yt_ready, i + 1)
                pool.indirect_dma_start(y_rows, bass.IndirectOffsetOnAxis(pair_u[:, i:i + 1], 0),
                                        yt[:, i % 2, :], None).then_inc(rows_scattered[i % 2], 16)

            pool.wait_ge(indices_ready, 2)
            for q in range(4):
                pool.wait_ge(xn_stored[q], 16 * (NB // 4))
            AHEAD = 4
            for i in range(AHEAD):
                gather(i)
            for i in range(NT):
                scatter(i)
                if i + AHEAD < NT:
                    gather(i + AHEAD)

        @block.scalar
        def _(act):
            for c in range(NCH):
                act.dma_start(v_rows[:, 2 * c:2 * c + 2, :], v_dram[:, 2 * c:2 * c + 2, :]).then_inc(v_in[c], 16)
                if c == 0:
                    with nc.allow_non_contiguous_dma(reason="two columns of 128 words"):
                        act.dma_start(cols[:, 0, :], decay.rearrange("(c p) -> p c", p=P)).then_inc(small_in, 16)
                        act.dma_start(cols[:, 1, :], first.rearrange("(c p) -> p c", p=P)).then_inc(small_in, 16)
                    act.dma_start(gates[:, 0:1], g_xattn.rearrange("(a b) -> a b", a=1).to_broadcast([P, 1])).then_inc(small_in, 16)
                    act.dma_start(gates[:, 1:2], g_ffn.rearrange("(a b) -> a b", a=1).to_broadcast([P, 1])).then_inc(small_in, 16)
            act.wait_ge(small_in, 16 * 5)
            act.activation(tg[:], gates[:], ACT.Tanh).then_inc(gates_ready, 1)
            act.activation(wcol[:], cols[:, 0, :], ACT.Exp).then_inc(gates_ready, 1)
            act.wait_ge(gate_turned, 1)
            act.activation(gate_t[:], bank_h[:, 0:DC * NE].rearrange("p (c e) -> p c e", c=DC),
                           ACT.Copy).then_inc(gate_ready, 1)
            act.wait_ge(pads_ready, 1)

            def move_kv(b):
                c = b // 2
                act.wait_ge(in_turned, b + 1)
                if c >= 2:
                    act.wait_ge(yw_ready, c - 1)
                act.activation(kv[:, c % 2, :, DC * (b % 2):DC * (b % 2) + DC, 1:TP],
                               bank_in[:, b % 2, :].rearrange("p (k s t) -> p k s t", k=2, s=DC),
                               ACT.Copy).then_inc(kv_ready, 1)

            def exps(c):
                act.wait_ge(args_ready, c + 1)
                e = ex[:, c % 2]
                act.activation(e[:, 0:2, :, 1:TP], e[:, 0:2, :, 1:TP], ACT.Exp).then_inc(exps_ready, 1)
                act.activation(e[:, 2:4, :, 1:TP], e[:, 2:4, :, 1:TP], ACT.Exp, scale=-1.0).then_inc(exps_ready, 1)

            def move_xnT(b):
                act.wait_ge(xn_turned, b + 1)
                if b >= 2:
                    act.wait_ge(sgu_ready, b - 1)
                act.activation(xnT[:, b % 2], bank_x[:, 0:DC * P].rearrange("p (c t) -> p c t", c=DC),
                               ACT.Copy).then_inc(xnT_ready, 1)

            def shared_tanh(b):
                act.wait_ge(sgu_ready, b + 1)
                if b >= 2:
                    act.wait_ge(hs_ready, b - 1)
                act.activation(th[:, b % 2], bank_g[:, 0, 0:SJ], ACT.Tanh, scale=0.5).then_inc(sth_ready, 1)

            def move_hsT(b):
                act.wait_ge(hs_turned, b + 1)
                if b >= 2:
                    act.wait_ge(sy_ready, b - 1)
                full = SJ // P
                act.activation(hsT[:, b % 2, 0:full, :], bank_h[:, 0:full * P].rearrange("p (k t) -> p k t", t=P),
                               ACT.Copy).then_inc(hsT_ready, 1)
                rest = SCH[full][1]
                act.activation(hsT[0:rest, b % 2, full, :], bank_h[0:rest, full * P:(full + 1) * P],
                               ACT.Copy).then_inc(hsT_ready, 1)

            for b in range(4):
                move_kv(b)
            exps(0)
            for c in range(NCH):
                if c + 1 < NCH:
                    exps(c + 1)
                if c >= 1:
                    shared_tanh(2 * c - 2)
                    move_hsT(2 * c - 2)
                    shared_tanh(2 * c - 1)
                if c + 2 < NCH:
                    move_kv(2 * c + 4)
                    move_kv(2 * c + 5)
                if c >= 1:
                    move_hsT(2 * c - 1)
                move_xnT(2 * c)
                move_xnT(2 * c + 1)
            shared_tanh(NB - 2)
            move_hsT(NB - 2)
            shared_tanh(NB - 1)
            move_hsT(NB - 1)
            act.wait_ge(esub_ready, 2)
            act.activation(esub[:], esub[:], ACT.Exp).then_inc(eexp_ready, 1)
            act.activation(etop[:], etop[:], ACT.Exp).then_inc(eexp_ready, 1)

            def silu(i, par):
                act.wait_ge(gu_ready, i + 1)
                act.activation(sg[:, par, :], gu_bank[par][:, 0:J], ACT.Silu).then_inc(sg_ready, 1)

            def move_y(i, par, reused):
                act.wait_ge(y_ready, i + 1)
                if reused is not None:
                    act.wait_ge(rows_scattered[par], reused)
                act.activation(yt[:, par, :], yo_bank[par][:, 0:D], ACT.Copy).then_inc(yt_ready, 1)

            silu(0, 0)
            silu(1, 1)
            move_y(0, 0, None)
            silu(2, 0)
            move_y(1, 1, None)
            with act.Fori(0, (NT - 3) // 2) as r:
                silu(2 * r + 3, 1)
                move_y(2 * r + 2, 0, 16 * r + 16)
                silu(2 * r + 4, 0)
                move_y(2 * r + 3, 1, 16 * r + 16)
            move_y(NT - 1, 0, 16 * ((NT - 1) // 2))

        @block.tensor
        def _(pe):
            pe.wait_ge(consts_ready, 1)
            pe.wait_ge(small_in, 16 * 5)
            for k in range(DC):
                mm = pe.transpose(bank_h[:, k * NE:(k + 1) * NE], gate_rows[:, k * P:(k + 1) * P], ident[0:NE, 0:NE])
            mm.then_inc(gate_turned, 1)

            def turn_in(b):
                c = b // 2
                pe.wait_ge(kn_ready, c + 1)
                pe.wait_ge(v_in[c], 16)
                if b >= 2:
                    pe.wait_ge(kv_ready, b - 1)
                for s, rows in enumerate((kn, v_rows)):
                    for k in range(DC):
                        at = (s * DC + k) * P
                        mm = pe.transpose(bank_in[:, b % 2, at:at + P], rows[:, b, k * P:(k + 1) * P], ident[:])
                mm.then_inc(in_turned, 1)

            def turn_yw(b):
                c = b // 2
                pe.wait_ge(yw_ready, c + 1)
                if b >= 1:
                    pe.wait_ge(x1_ready, b)
                for k in range(DC):
                    mm = pe.transpose(bank_y[:, k * P:(k + 1) * P], yw[:, c % 2, DC * (b % 2) + k, :], ident[:])
                mm.then_inc(yw_turned, 1)

            def turn_xn(b):
                pe.wait_ge(xn_ready, b + 1)
                if b >= 1:
                    pe.wait_ge(xnT_ready, b)
                if b >= 2:
                    pe.wait_ge(sy_added, b - 1 if b % 2 == 0 else b - 2)
                for k in range(DC):
                    mm = pe.transpose(bank_x[:, k * P:(k + 1) * P], xn[:, b % 4, k * P:(k + 1) * P], ident[:])
                mm.then_inc(xn_turned, 1)

            def logits(b):
                pe.wait_ge(xnT_ready, b + 1)
                if b == 0:
                    pe.wait_ge(gate_ready, 1)
                for k in range(DC):
                    mm = pe.matmul(bank_l[:, b * NE:(b + 1) * NE], xnT[:, b % 2, k, :], gate_t[:, k, :],
                                   start=(k == 0), stop=(k == DC - 1))
                mm.then_inc(logits_ready, 1)

            def shared_up(b):
                if b == 0:
                    pe.wait_ge(shared_in, 16 * (1 + len(SCH)))
                if b >= 1:
                    pe.wait_ge(hs_ready, b)
                for n in range(2):
                    for k in range(DC):
                        mm = pe.matmul(bank_g[:, n, 0:SJ], xnT[:, b % 2, k, :], s_gu[:, k, n * SJ:(n + 1) * SJ],
                                       start=(k == 0), stop=(k == DC - 1))
                mm.then_inc(sgu_ready, 1)

            def turn_hs(b):
                pe.wait_ge(hs_ready, b + 1)
                if b >= 1:
                    pe.wait_ge(hsT_ready, 2 * b)
                for k, (at, n) in enumerate(SCH):
                    mm = pe.transpose(bank_h[0:n, k * P:(k + 1) * P], hs[:, b % 2, at:at + n], ident[:])
                mm.then_inc(hs_turned, 1)

            def shared_down(b):
                pe.wait_ge(hsT_ready, 2 * b + 2)
                if b >= 1:
                    pe.wait_ge(sy_added, b)
                for k, (at, n) in enumerate(SCH):
                    mm = pe.matmul(bank_x[:, DC * P:DC * P + D], hsT[0:n, b % 2, k, :], s_dn[0:n, k, :],
                                   start=(k == 0), stop=(k == len(SCH) - 1))
                mm.then_inc(sy_ready, 1)

            for b in range(4):
                turn_in(b)
            for c in range(NCH):
                if c >= 1:
                    shared_up(2 * c - 2)
                turn_yw(2 * c)
                turn_yw(2 * c + 1)
                if c >= 1:
                    turn_hs(2 * c - 2)
                    shared_down(2 * c - 2)
                    shared_up(2 * c - 1)
                if c + 2 < NCH:
                    turn_in(2 * c + 4)
                    turn_in(2 * c + 5)
                if c >= 1:
                    turn_hs(2 * c - 1)
                    shared_down(2 * c - 1)
                for b in (2 * c, 2 * c + 1):
                    turn_xn(b)
                    logits(b)
            shared_up(NB - 2)

            pe.wait_ge(both_ready, 1)
            pe.wait_ge(consts_ready, 11)
            pe.matmul(bank_l[:, 0:(NB + 1) * NE], tri[:], both[:].rearrange("p b e -> p (b e)"), start=True, stop=False)
            for b in range(NB):
                mm = pe.matmul(bank_l[:, (b + 1) * NE:(NB + 1) * NE].rearrange("p (b e) -> p b e", e=NE), ones[:],
                               both[:, b:b + 1, :].to_broadcast([P, NB - b, NE]), start=False, stop=(b == NB - 1))
            mm.then_inc(ranks_ready, 1)
            turn_hs(NB - 2)
            shared_down(NB - 2)
            shared_up(NB - 1)
            pe.wait_ge(hot_ready, 1)
            for q in range(2 * NB):
                pe.wait_ge(hot_ready, q + 2)
                mm = pe.matmul(bank_y[:, 0:NTP], row_hot[:, q, :], tile_val[:, q, :], start=(q == 0), stop=(q == 2 * NB - 1))
            mm.then_inc(table_ready, 1)
            turn_hs(NB - 1)
            shared_down(NB - 1)

            def turn_x(i, par, q4, landed, reused=True):
                pe.wait_ge(rows_gathered[q4], landed)
                if reused:
                    pe.wait_ge(xgT_ready, i - 1)
                for k in range(DC):
                    mm = pe.transpose(t_bank[par][:, k * P:(k + 1) * P],
                                      xg[:, q4, k * P:(k + 1) * P], ident[:])
                mm.then_inc(xg_turned, 1)

            def gate_up(i, par, expert, reused=True):
                pe.wait_ge(xgT_ready, i + 1)
                if reused:
                    pe.wait_ge(h_ready, i - 1)
                for k in range(DC):
                    mm = pe.matmul(gu_bank[par][:, 0:J2], xgT[:, par, k, :],
                                   w_gu[:, bass.ds(expert, 1), k, :].rearrange("p a j -> p (a j)"),
                                   start=(k == 0), stop=(k == DC - 1))
                mm.then_inc(gu_ready, 1)

            def turn_h(i, par, reused=True):
                pe.wait_ge(h_ready, i + 1)
                if reused:
                    pe.wait_ge(hT_ready, i - 1)
                for k in range(2):
                    mm = pe.transpose(ht_bank[par][0:JH, k * P:(k + 1) * P], h[:, par, k * JH:(k + 1) * JH], ident[:])
                mm.then_inc(h_turned, 1)

            def down(i, par, expert, reused=True):
                pe.wait_ge(hT_ready, i + 1)
                if reused:
                    pe.wait_ge(yt_ready, i - 1)
                for k in range(2):
                    mm = pe.matmul(yo_bank[par][:, 0:D], hT[:, par, k, :],
                                   w_dn[:, bass.ds(expert, 1), k, :].rearrange("p a d -> p (a d)"),
                                   start=(k == 0), stop=(k == 1))
                mm.then_inc(y_ready, 1)

            def owner_of(i):
                return pe.value_load(owner[0:1, bass.ds(i, 1)], min_val=0, max_val=NE - 1)

            pe.wait_ge(owner_ready, 1)
            pe.wait_ge(experts_in, 16 * 8)
            pe.wait_ge(sy_added, NB)
            turn_x(0, 0, 0, 16, reused=False)
            gate_up(0, 0, owner_of(0), reused=False)
            turn_x(1, 1, 1, 16, reused=False)
            turn_h(0, 0, reused=False)
            for i in (1, 2):
                gate_up(i, i % 2, owner_of(i), reused=(i >= 2))
                turn_x(i + 1, (i + 1) % 2, (i + 1) % 4, 16)
                down(i - 1, (i - 1) % 2, owner_of(i - 1), reused=False)
                turn_h(i, i % 2, reused=(i >= 2))
            with pe.Fori(0, (NT - 7) // 4) as r:
                for u in range(4):
                    i = 4 * r + (3 + u)
                    gate_up(i, (3 + u) % 2, owner_of(i))
                    turn_x(i + 1, u % 2, u % 4, 16 * r + 32)
                    down(i - 1, u % 2, owner_of(i - 1))
                    turn_h(i, (3 + u) % 2)
            for i in range(NT - 4, NT):
                gate_up(i, i % 2, owner_of(i))
                if i + 1 < NT:
                    turn_x(i + 1, (i + 1) % 2, (i + 1) % 4, 16 * ((i + 1) // 4 + 1))
                down(i - 1, (i - 1) % 2, owner_of(i - 1))
                turn_h(i, i % 2)
            down(NT - 1, (NT - 1) % 2, owner_of(NT - 1))

        @block.vector
        def _(dve):
            steps = [0]

            def do(ins):
                steps[0] += 1
                ins.then_inc(dve_step, 1)

            def settle():
                dve.wait_ge(dve_step, steps[0])

            do(dve.memset(kv[:, :, 0, :, 0:1], NEG))
            do(dve.memset(decay_t[:], 0.0))
            do(dve.memset(ex[:, :, :, :, 0:1].rearrange("p a k s o -> p (a k) (s o)"), 0.0))
            do(dve.memset(vb[:, :, 0:1], 0.0))
            settle()
            do(dve.memset(decay_t[:, :, 0:1], NEG))
            settle()

            def variance(b):
                dve.bn_stats(stats[:, b, :], x1[:, b, :]).then_inc(dve_step, 1)
                steps[0] += 1
                settle()
                do(dve.bn_aggr(mv[:, b, :], stats[:, b, :]))

            def publish_variance(c):
                settle()
                dve.tensor_scalar(vpe[:, 2 * c:2 * c + 2], mv[:, 2 * c:2 * c + 2, 1], EPS, None,
                                  ALU.add).then_inc(var_ready, 1)

            for c in range(NCH):
                dve.wait_ge(x_in[c], 16)
                variance(2 * c)
                variance(2 * c + 1)
                publish_variance(c)
                if c == 0:
                    dve.wait_ge(gates_ready, 2)
                    do(dve.tensor_scalar(wcol[:], wcol[:], -1.0, None, ALU.mult))
                    settle()
                    for k in range(DC):
                        ins = dve.tensor_scalar(decay_t[:, k:SEQ:DC, 1:TP], decay_t[:, k:SEQ:DC, 1:TP], wcol[:, k:k + 1],
                                                None, ALU.add)
                        if k == DC - 1:
                            ins.then_inc(pads_ready, 1)
                        else:
                            do(ins)
            for c in range(NCH):
                dve.wait_ge(rstd_ready, c + 1)
                for b in (2 * c, 2 * c + 1):
                    ins = dve.tensor_scalar(kn[:, b, :], x1[:, b, :], mv[:, b, 0:1], rstd[:, 0, b:b + 1],
                                            ALU.subtract, ALU.mult)
                    if b % 2:
                        ins.then_inc(kn_ready, 1)
                    else:
                        do(ins)
            settle()
            dve.wait_ge(pads_ready, 1)

            def arguments(c):
                par = c % 2
                dve.wait_ge(kv_ready, 2 * c + 2)
                k_all = kv[:, par, 0].rearrange("p s t -> p (s t)")
                do(dve.tensor_tensor_scan(pp[:, par].rearrange("p s t -> p (s t)"),
                                          decay_t[:].rearrange("p s t -> p (s t)"), k_all, NEG, ALU.add, ALU.max))
                settle()
                do(dve.tensor_tensor(diff, pp[:, par, :, 0:T], kv[:, par, 0, :, 1:TP], ALU.subtract))
                settle()
                if c >= 2:
                    dve.wait_ge(e2v_ready, c - 1)
                for k in range(DC):
                    a = diff[:, k:SEQ:DC, :]
                    u, w = cols[:, 1, k:k + 1], wcol[:, k:k + 1]
                    for kind, (op, s, cut) in enumerate(((ALU.subtract, u, ALU.min), (ALU.add, w, ALU.min),
                                                         (ALU.subtract, u, ALU.max), (ALU.add, w, ALU.max))):
                        ins = dve.tensor_scalar(ex[:, par, kind, k:SEQ:DC, 1:TP], a, s, 0.0, op, cut)
                        if k == DC - 1 and kind == 3:
                            ins.then_inc(args_ready, 1)
                        else:
                            do(ins)
                settle()
                dve.wait_ge(args_ready, c + 1)

            def recurrence(c):
                par = c % 2
                e1, e1b, e2, e2b = (ex[:, par, k] for k in range(4))
                v = kv[:, par, 1, :, 1:TP]
                flat = "p s t -> p (s t)"
                dve.wait_ge(exps_ready, 2 * c + 2)
                do(dve.tensor_tensor(vb[:, :, 1:TP], e2b[:, :, 1:TP], v, ALU.mult))
                do(dve.tensor_tensor_scan(bb[:].rearrange(flat), e1b.rearrange(flat), e2b.rearrange(flat), 0.0,
                                          ALU.mult, ALU.add))
                settle()
                do(dve.tensor_tensor_scan(aa[:].rearrange(flat), e1b.rearrange(flat), vb[:].rearrange(flat), 0.0,
                                          ALU.mult, ALU.add))
                do(dve.tensor_tensor(den, e1[:, :, 1:TP], bb[:, :, 0:T], ALU.mult))
                settle()
                do(dve.tensor_tensor(num, e1[:, :, 1:TP], aa[:, :, 0:T], ALU.mult))
                do(dve.tensor_tensor(den, den, e2[:, :, 1:TP], ALU.add))
                settle()
                dve.wait_ge(e2v_ready, c + 1)
                do(dve.tensor_tensor(num, num, e2v[:, par], ALU.add))
                do(dve.reciprocal(den, den))
                settle()
                if c >= 2:
                    dve.wait_ge(yw_turned, 2 * c - 2)
                dve.tensor_tensor(yw[:, par], num, den, ALU.mult).then_inc(yw_ready, 1)

            def add_yw(b):
                dve.wait_ge(yw_turned, b + 1)
                dve.scalar_tensor_tensor(x1[:, b, :], bank_y[:, 0:D], tg[:, 0:1], x1[:, b, :], ALU.mult,
                                         ALU.add).then_inc(x1_ready, 1)
                dve.wait_ge(x1_ready, b + 1)
                variance(b)

            def normalise(b):
                if b % 2 == 0:
                    dve.wait_ge(rstd_ready, NCH + b // 2 + 1)
                if b >= 4:
                    dve.wait_ge(xn_stored[b % 4], 16 * (b // 4))
                    dve.wait_ge(xn_turned, b - 3)
                dve.tensor_scalar(xn[:, b % 4, :], x1[:, b, :], mv[:, b, 0:1], rstd[:, 1, b:b + 1],
                                  ALU.subtract, ALU.mult).then_inc(xn_ready, 1)

            def shared_h(b):
                par = b % 2
                dve.wait_ge(sth_ready, b + 1)
                if b >= 2:
                    dve.wait_ge(hs_turned, b - 1)
                do(dve.scalar_tensor_tensor(hs[:, par], th[:, par], 1.0, bank_g[:, 0, 0:SJ], ALU.add, ALU.mult))
                settle()
                dve.scalar_tensor_tensor(hs[:, par], bank_g[:, 1, 0:SJ], 0.5, hs[:, par], ALU.mult,
                                         ALU.mult).then_inc(hs_ready, 1)

            def add_shared(b):
                dve.wait_ge(sy_ready, b + 1)
                dve.scalar_tensor_tensor(x1[:, b, :], bank_x[:, DC * P:DC * P + D], tg[:, 1:2], x1[:, b, :], ALU.mult,
                                         ALU.add).then_inc(sy_added, 1)

            arguments(0)
            for c in range(NCH):
                if c + 1 < NCH:
                    arguments(c + 1)
                recurrence(c)
                if c >= 1:
                    shared_h(2 * c - 2)
                add_yw(2 * c)
                add_yw(2 * c + 1)
                publish_variance(c)
                if c >= 1:
                    add_shared(2 * c - 2)
                    shared_h(2 * c - 1)
                    add_shared(2 * c - 1)
                normalise(2 * c)
                normalise(2 * c + 1)

            dve.wait_ge(logits_ready, NB)
            do(dve.tensor_copy(lg[:].rearrange("p b e -> p (b e)"), bank_l[:, 0:NB * NE]))
            settle()
            for b in range(NB):
                do(dve.max(top[:, b, :], lg[:, b, :]))
            settle()
            for b in range(NB):
                do(dve.max_index(topi[:, b, :], top[:, b, :], lg[:, b, :]))
            settle()
            dve.wait_ge(consts_ready, 11)
            for k in range(2):
                do(dve.tensor_tensor(mask[:, k], iota_e[:].unsqueeze(1).to_broadcast([P, NB, NE]),
                                     topi[:, :, k:k + 1].to_broadcast([P, NB, NE]), ALU.is_equal))
            settle()
            dve.tensor_tensor(both[:, 0:NB, :], mask[:, 0], mask[:, 1], ALU.add).then_inc(both_ready, 1)
            shared_h(NB - 2)
            dve.wait_ge(ranks_ready, 1)
            total = bank_l[:, NB * NE:(NB + 1) * NE]
            do(dve.tensor_tensor(over[:], total.unsqueeze(2).to_broadcast([P, NE, NB]),
                                 limits[:].unsqueeze(1).to_broadcast([P, NE, NB]), ALU.is_gt))
            settle()
            do(dve.tensor_reduce(tiles[:], over[:], AX.X, ALU.add))
            settle()
            do(dve.tensor_tensor_scan(ends[:], ones_f[:], tiles[:], 0.0, ALU.mult, ALU.add))
            settle()
            do(dve.tensor_tensor(begins[:], ends[:], tiles[:], ALU.subtract))
            settle()
            do(dve.scalar_tensor_tensor(slot_e[:], begins[:].unsqueeze(1).to_broadcast([P, NB, NE]), float(P),
                                        bank_l[:, 0:NB * NE].rearrange("p (b e) -> p b e", e=NE), ALU.mult, ALU.add))
            settle()
            for k in range(2):
                do(dve.tensor_tensor(slot_m[:, k], mask[:, k], slot_e[:], ALU.mult))
            settle()
            do(dve.tensor_reduce(slot[:], slot_m[:].rearrange("p k b e -> p (k b) e"), AX.X, ALU.add))
            settle()
            do(dve.tensor_copy(slot_u[:], slot[:]))
            settle()
            do(dve.tensor_single_scalar(row_u[:], slot_u[:], P - 1, ALU.bitwise_and))
            do(dve.tensor_single_scalar(tile_u[:], slot_u[:], 7, ALU.logical_shift_right))
            settle()
            do(dve.tensor_copy(row_f[:], row_u[:]))
            do(dve.tensor_tensor(tile_hot[:], iota_t[:].unsqueeze(1).to_broadcast([P, 2 * NB, NTP]),
                                 tile_u[:].unsqueeze(2).to_broadcast([P, 2 * NB, NTP]), ALU.is_equal))
            settle()
            dve.tensor_tensor(tile_val[:], tile_hot[:], pair_no[:].unsqueeze(2).to_broadcast([P, 2 * NB, NTP]),
                              ALU.mult).then_inc(hot_ready, 1)
            for q in range(2 * NB):
                dve.tensor_scalar(row_hot[:, q, :], iota_r[:], row_f[:, q:q + 1], None,
                                  ALU.is_equal).then_inc(hot_ready, 1)
            do(dve.tensor_tensor(before[:], ends[0:1, :].unsqueeze(1).to_broadcast([1, NTP, NE]),
                                 iota_t[0:1, :].unsqueeze(2).to_broadcast([1, NTP, NE]), ALU.is_le))
            settle()
            do(dve.tensor_reduce(owner_f[:], before[:], AX.X, ALU.add))
            settle()
            dve.tensor_scalar(owner[:], owner_f[:], float(NE - 1), None, ALU.min).then_inc(owner_ready, 1)
            dve.wait_ge(table_ready, 1)
            do(dve.scalar_tensor_tensor(pad_val[:], bank_y[:, 0:NTP], 0.0, pad_row[:], ALU.is_equal, ALU.mult))
            settle()
            dve.scalar_tensor_tensor(pair_u[:], bank_y[:, 0:NTP], -1.0, pad_val[:], ALU.add,
                                     ALU.add).then_inc(indices_ready, 1)
            dve.wait_ge(indices_ready, 1)
            dve.tensor_single_scalar(token_u[:], pair_u[:], NTOK - 1, ALU.bitwise_and).then_inc(indices_ready, 1)
            add_shared(NB - 2)
            shared_h(NB - 1)
            dve.tensor_tensor(esub[:], lg[:], top[:, :, 0:1].to_broadcast([P, NB, NE]),
                              ALU.subtract).then_inc(esub_ready, 1)
            dve.tensor_tensor(etop[:], top[:, :, 1], top[:, :, 0], ALU.subtract).then_inc(esub_ready, 1)
            add_shared(NB - 1)
            dve.wait_ge(eexp_ready, 2)
            do(dve.tensor_reduce(esum[:], esub[:], AX.X, ALU.add))
            settle()
            do(dve.reciprocal(esum[:], esum[:]))
            settle()
            do(dve.tensor_scalar(wts[:, 0], esum[:], tg[:, 1:2], None, ALU.mult))
            settle()
            do(dve.tensor_tensor(wts[:, 1], wts[:, 0], etop[:], ALU.mult))
            settle()

            def move_x(i, par):
                dve.wait_ge(xg_turned, i + 1)
                dve.tensor_copy(xgT[:, par].rearrange("p c t -> p (c t)"), t_bank[par][:, 0:DC * P]).then_inc(xgT_ready, 1)

            def gated(i, par):
                dve.wait_ge(sg_ready, i + 1)
                dve.tensor_tensor(h[:, par, :], sg[:, par, :], gu_bank[par][:, J:J2], ALU.mult).then_inc(h_ready, 1)

            def move_h(i, par):
                dve.wait_ge(h_turned, i + 1)
                dve.tensor_copy(hT[:, par].rearrange("p c t -> p (c t)"), ht_bank[par][0:JH, 0:2 * P]).then_inc(hT_ready, 1)

            move_x(0, 0)
            move_x(1, 1)
            gated(0, 0)
            for i in (1, 2):
                move_h(i - 1, (i - 1) % 2)
                dve.wait_ge(gu_ready, i)
                move_x(i + 1, (i + 1) % 2)
                gated(i, i % 2)
            with dve.Fori(0, (NT - 3) // 2 - 1) as r:
                for u in range(2):
                    i = 2 * r + (3 + u)
                    dve.wait_ge(y_ready, i - 2)
                    move_h(i - 1, u)
                    dve.wait_ge(gu_ready, i)
                    move_x(i + 1, u)
                    dve.wait_ge(h_turned, i - 1)
                    gated(i, 1 - u)
            for i in range(NT - 2, NT):
                dve.wait_ge(y_ready, i - 2)
                move_h(i - 1, (i - 1) % 2)
                if i + 1 < NT:
                    dve.wait_ge(gu_ready, i)
                    move_x(i + 1, (i + 1) % 2)
                dve.wait_ge(h_turned, i - 1)
                gated(i, i % 2)
            dve.wait_ge(y_ready, NT - 2)
            move_h(NT - 1, (NT - 1) % 2)

            for b in range(NB):
                dve.wait_ge(y_back[b], 16)
                do(dve.scalar_tensor_tensor(x1[:, b, :], y2[:, b, 0, :], wts[:, 0, b:b + 1], x1[:, b, :], ALU.mult,
                                            ALU.add))
                settle()
                dve.scalar_tensor_tensor(x1[:, b, :], y2[:, b, 1, :], wts[:, 1, b:b + 1], x1[:, b, :], ALU.mult,
                                         ALU.add).then_inc(out_ready, 1)


_INS = ['x', 'ctx_2048', 'g_xattn', 'g_ffn', 'L0_xattn_time_decay', 'L0_xattn_time_first', 'L0_ffn_gate_w',
        'L0_ffn_w_gate_up', 'L0_ffn_w_down', 'L0_ffn_shared_gate_up', 'L0_ffn_shared_down']


def kernel(**inputs):
    import numpy as np
    import concourse.bacc as bacc
    from concourse.bass_utils import run_bass_kernel_spmd

    nc = bacc.Bacc("TRN2", target_bir_lowering=False, num_devices=1)
    arrays, args = {}, []
    for name in _INS:
        a = np.ascontiguousarray(inputs[name])
        arrays[f"in_{name}"] = a
        args.append(nc.dram_tensor(f"in_{name}", a.shape, mybir.dt.from_np(a.dtype), kind="ExternalInput").ap())
    out = nc.dram_tensor("out", inputs['x'].shape, F32, kind="ExternalOutput").ap()
    gated_wkv_moe(nc, *args, out)
    r = run_bass_kernel_spmd(nc, [arrays], core_ids=[0])
    return r.results[0]["out"]
```

```python
from contextlib import ExitStack

import concourse.bass as bass
from concourse import mybir

ALU = mybir.AluOpType
ACT = mybir.ActivationFunctionType
AX = mybir.AxisListType
F32 = mybir.dt.float32
F16 = mybir.dt.float16
BF16 = mybir.dt.bfloat16
U32 = mybir.dt.uint32
I32 = mybir.dt.int32

P = 128
EPS = 1e-5
NEG = -1e38


def gated_wkv_moe(nc, x, ctx_in, g_xattn, g_ffn, decay, first, gate_w, w_gate_up, w_down, s_gate_up, s_down, out):
    NB, T, D = x.shape
    NE, _, J2 = w_gate_up.shape
    J = J2 // 2
    S2 = s_gate_up.shape[1]
    SJ = S2 // 2
    NTOK = NB * T
    DC = D // P
    JH = J // 2
    PAIRS = 2 * NTOK
    NT = PAIRS // P + NE - 1
    NTP = 32
    SEQ = 2 * DC
    TP = T + 1
    NCH = NB // 2
    LAST = [NB - 2, NB - 1]
    SCH = [(k * P, min(P, SJ - k * P)) for k in range((SJ + P - 1) // P)]
    assert T == P and DC == 2 and NT < NTP and JH <= P and PAIRS <= 2048

    xn_rows = nc.dram_tensor("xn_rows", (NTOK, D), F32, kind="Internal").ap()
    y_rows = nc.dram_tensor("y_rows", (PAIRS + NT * P, D), F32, kind="Internal").ap()

    with ExitStack() as ctx:
        def sb(name, shape, dt=F32):
            return ctx.enter_context(nc.sbuf_tensor(name, shape, dt))

        def psum(name, shape, dt=F32):
            return ctx.enter_context(nc.psum_tensor(name, shape, dt))

        def sem(name):
            return ctx.enter_context(nc.semaphore(name))

        w_gu = sb("w_gu", [P, NE, DC, J2])
        w_dn = sb("w_dn", [JH, NE, 2, D])
        s_gu = sb("s_gu", [P, DC, S2])
        s_dn = sb("s_dn", [P, len(SCH), D])
        gate_rows = sb("gate_rows", [NE, D])
        gate_t = sb("gate_t", [P, DC, NE])
        x1 = sb("x1", [P, NB, D])
        xg = sb("xg", [P, NTP, D])
        kn = xg[:, 0:NB, :]
        v_rows = xg[:, NB:2 * NB, :]
        wk = xg[:, 2 * NB:NTP, :].rearrange("p n d -> p (n d)").rearrange("p (q s t) -> p q s t", s=SEQ, t=T)
        yw, e2v, num, den, diff = wk[:, 0:2], wk[:, 2:4], wk[:, 4], wk[:, 5], wk[:, 6:8]
        y2 = xg[:, 0:2 * NB, :].rearrange("p (b k) d -> p b k d", k=2)
        xn = sb("xn", [P, 4, D])
        stats = sb("stats", [P, NB, 6])
        mv = sb("mv", [P, NB, 2])
        vpe = sb("vpe", [P, NB])
        rstd = sb("rstd", [P, 2, NB])
        neg_half = sb("neg_half", [P, NB])
        kv = sb("kv", [P, NCH, 2, SEQ, TP])
        pp = sb("pp", [P, 2, SEQ, TP])
        ex = sb("ex", [P, 2, 4, SEQ, TP])
        vb = sb("vb", [P, SEQ, TP])
        aa = sb("aa", [P, SEQ, TP])
        bb = sb("bb", [P, SEQ, TP])
        decay_t = sb("decay_t", [P, SEQ, TP])
        cols = sb("cols", [P, 2, DC])
        wcol = sb("wcol", [P, DC])
        neg_cols = sb("neg_cols", [P, 2, DC])
        shift = sb("shift", [P, 2, NB])
        gates = sb("gates", [P, 2])
        tg = sb("tg", [P, 2])
        xnT = sb("xnT", [P, NB, DC, P])
        th = sb("th", [P, 2, SJ])
        hs = sb("hs", [P, 2, SJ])
        hsT = sb("hsT", [P, 2, len(SCH), P])
        lg = sb("lg", [P, NB, NE])
        top = sb("top", [P, NB, 8])
        topi = sb("topi", [P, NB, 8], U32)
        mask = sb("mask", [P, 2, NB, NE], BF16)
        both = sb("both", [P, NB + 1, NE], BF16)
        tiles = sb("tiles", [P, NE])
        ends = sb("ends", [P, NE])
        begins = sb("begins", [P, NE])
        slot = sb("slot", [P, 2 * NB])
        slot_u = sb("slot_u", [P, 2 * NB], U32)
        row_u = sb("row_u", [P, 2 * NB], U32)
        tile_u = sb("tile_u", [P, 2 * NB], U32)
        row_f = sb("row_f", [P, 2 * NB])
        free = ex[:].rearrange("p a k s t -> p (a k s t)")
        hot_words, tile_words = 2 * NB * P // 2, 2 * NB * NTP // 2
        row_hot = free[:, 0:hot_words].bitcast(F16).rearrange("p (q r) -> p q r", r=P)
        tile_hot = free[:, hot_words:hot_words + tile_words].bitcast(F16).rearrange("p (q i) -> p q i", i=NTP)
        tile_val = free[:, hot_words + tile_words:hot_words + 2 * tile_words].bitcast(F16).rearrange("p (q i) -> p q i", i=NTP)
        at = hot_words + 2 * tile_words
        over = free[:, at:at + NE * NB].rearrange("p (e b) -> p e b", b=NB)
        at += NE * NB
        slot_e = free[:, at:at + NB * NE].rearrange("p (b e) -> p b e", e=NE)
        at += NB * NE
        slot_m = free[:, at:at + 2 * NB * NE].rearrange("p (k b e) -> p k b e", k=2, e=NE)
        at += 2 * NB * NE
        ended = free[0:1, at:at + NTP * NE].rearrange("p (i e) -> p i e", e=NE)
        at += NTP * NE
        esub = free[:, at:at + NB * NE].rearrange("p (b e) -> p b e", e=NE)
        pad_val = sb("pad_val", [P, NTP])
        pair_u = sb("pair_u", [P, NTP], U32)
        token_u = sb("token_u", [P, NTP], U32)
        owner_f = sb("owner_f", [1, NTP])
        owner = sb("owner", [1, NTP], I32)
        etop = sb("etop", [P, NB])
        esum = sb("esum", [P, NB])
        wts = sb("wts", [P, 2, NB])
        xgT = sb("xgT", [P, 2, DC, P])
        sg = sb("sg", [P, 2, J])
        h = sb("h", [P, 2, J])
        hT = sb("hT", [JH, 2, 2, P])
        yt = sb("yt", [P, 2, D])
        ident = sb("ident", [P, P])
        tri = sb("tri", [P, P], BF16)
        ones = sb("ones", [P, P], BF16)
        ones_f = sb("ones_f", [P, NE])
        iota_e = sb("iota_e", [P, NE])
        iota_t = sb("iota_t", [P, NTP])
        iota_r = sb("iota_r", [P, P], F16)
        pair_no = sb("pair_no", [P, 2 * NB], F16)
        limits = sb("limits", [P, NB])
        pad_row = sb("pad_row", [P, NTP])

        bank_in = psum("bank_in", [P, 2, 512])
        bank_y = psum("bank_y", [P, 512])
        bank_x = psum("bank_x", [P, 512])
        bank_l = psum("bank_l", [P, 512])
        bank_g = psum("bank_g", [P, 2, 512])
        bank_h = psum("bank_h", [P, 512])

        x_in = [sem(f"x_in{c}") for c in range(NCH)]
        v_in = [sem(f"v_in{c}") for c in range(NCH)]
        small_in = sem("small_in")
        shared_in = sem("shared_in")
        experts_in = sem("experts_in")
        xn_stored = [sem(f"xn_stored{q}") for q in range(4)]
        rows_gathered = [sem(f"rows_gathered{q}") for q in range(4)]
        rows_scattered = [sem(f"rows_scattered{q}") for q in range(2)]
        y_back = [sem(f"y_back{b}") for b in range(NB)]
        out_stored = sem("out_stored")
        dve_step = sem("dve_step")
        pool_step = sem("pool_step")
        consts_ready = sem("consts_ready")
        gates_ready = sem("gates_ready")
        decay_ready = sem("decay_ready")
        var_ready = sem("var_ready")
        rstd_ready = sem("rstd_ready")
        kn_ready = sem("kn_ready")
        in_turned = sem("in_turned")
        kv_ready = sem("kv_ready")
        shift_ready = sem("shift_ready")
        diff_ready = sem("diff_ready")
        relu_done = sem("relu_done")
        exps_ready = sem("exps_ready")
        e2v_ready = sem("e2v_ready")
        yw_ready = sem("yw_ready")
        yw_turned = sem("yw_turned")
        x1_ready = sem("x1_ready")
        xn_ready = sem("xn_ready")
        xn_turned = sem("xn_turned")
        xnT_ready = sem("xnT_ready")
        gate_turned = sem("gate_turned")
        gate_ready = sem("gate_ready")
        logits_ready = sem("logits_ready")
        lg_ready = sem("lg_ready")
        sgu_ready = sem("sgu_ready")
        sth_ready = sem("sth_ready")
        hs_ready = sem("hs_ready")
        hs_turned = sem("hs_turned")
        hsT_ready = sem("hsT_ready")
        sy_ready = sem("sy_ready")
        sy_added = sem("sy_added")
        both_ready = sem("both_ready")
        ranks_ready = sem("ranks_ready")
        hot_ready = sem("hot_ready")
        table_ready = sem("table_ready")
        indices_ready = sem("indices_ready")
        owner_ready = sem("owner_ready")
        esub_ready = sem("esub_ready")
        eexp_ready = sem("eexp_ready")
        xg_turned = sem("xg_turned")
        xgT_ready = sem("xgT_ready")
        gu_ready = sem("gu_ready")
        sg_ready = sem("sg_ready")
        h_ready = sem("h_ready")
        h_turned = sem("h_turned")
        hT_ready = sem("hT_ready")
        y_ready = sem("y_ready")
        yt_ready = sem("yt_ready")
        out_ready = sem("out_ready")

        x_dram = x.rearrange("b t d -> t b d")
        v_dram = ctx_in.rearrange("b t d -> t b d")
        out_dram = out.rearrange("b t d -> t b d")
        xn_dram = xn_rows.rearrange("(b t) d -> t b d", t=P)
        y_dram = y_rows[0:PAIRS, :].rearrange("(k b t) d -> t b k d", t=P, k=2)
        wgu_dram = w_gate_up.rearrange("e (c p) j -> p e c j", p=P)
        wdn_dram = w_down.rearrange("e (c p) d -> p e c d", p=JH)
        t_bank = [bank_in[:, 0, :], bank_in[:, 1, :]]
        gu_bank = [bank_g[:, 0, :], bank_g[:, 1, :]]
        ht_bank = [bank_y, bank_x]
        sg_banks = [bank_g, bank_in]
        yo_bank = [bank_l, bank_h]

        block = ctx.enter_context(nc.Block())

        @block.sync
        def _(sp):
            for c in range(NCH):
                sp.dma_start(x1[:, 2 * c:2 * c + 2, :], x_dram[:, 2 * c:2 * c + 2, :]).then_inc(x_in[c], 16)
            sp.dma_start(gate_rows[:], gate_w).then_inc(small_in, 16)
            sp.dma_start(s_gu[:], s_gate_up.rearrange("(c p) j -> p c j", p=P)).then_inc(shared_in, 16)
            for k, (at, n) in enumerate(SCH):
                sp.dma_start(s_dn[0:n, k, :], s_down[at:at + n, :]).then_inc(shared_in, 16)
            for q in range(4):
                sp.dma_start(w_gu[:, 4 * q:4 * q + 4], wgu_dram[:, 4 * q:4 * q + 4]).then_inc(experts_in, 16)
                sp.dma_start(w_dn[:, 4 * q:4 * q + 4], wdn_dram[:, 4 * q:4 * q + 4]).then_inc(experts_in, 16)
            for b in range(NB):
                sp.wait_ge(xn_ready, b + 1)
                sp.dma_start(xn_dram[:, b, :], xn[:, b % 4, :]).then_inc(xn_stored[b % 4], 16)
            sp.wait_ge(rows_scattered[0], 16 * ((NT + 1) // 2))
            sp.wait_ge(rows_scattered[1], 16 * (NT // 2))
            sp.wait_ge(xg_turned, NT)
            for b in range(NB):
                sp.dma_start(y2[:, b], y_dram[:, b]).then_inc(y_back[b], 16)
            for b in range(NB):
                sp.wait_ge(out_ready, b + 1)
                sp.dma_start(out_dram[:, b, :], x1[:, b, :]).then_inc(out_stored, 16)
            sp.wait_ge(out_stored, 16 * NB)

        @block.gpsimd
        def _(pool):
            steps = [0]

            def do(ins):
                steps[0] += 1
                ins.then_inc(pool_step, 1)

            def settle():
                pool.wait_ge(pool_step, steps[0])

            do(pool.memset(ident[:], 0.0))
            do(pool.memset(tri[:], 1.0))
            settle()
            pool.affine_select(out=ident[:], in_=ident[:], compare_op=ALU.not_equal, fill=1.0, base=0,
                               pattern=[[-1, P]], channel_multiplier=1).then_inc(consts_ready, 1)
            do(pool.memset(neg_half[:], -0.5))
            settle()

            def rsqrt(which, c):
                pool.wait_ge(var_ready, NCH * which + c + 1)
                pair = slice(2 * c, 2 * c + 2)
                pool.tensor_tensor(rstd[:, which, pair], vpe[:, pair], neg_half[:, pair],
                                   ALU.pow).then_inc(rstd_ready, 1)

            for c in range(NCH):
                rsqrt(0, c)
            pool.affine_select(out=tri[:], in_=tri[:], compare_op=ALU.is_gt, fill=0.0, base=0,
                               pattern=[[1, P]], channel_multiplier=-1).then_inc(consts_ready, 1)
            pool.memset(ones[:], 1.0).then_inc(consts_ready, 1)
            pool.memset(ones_f[:], 1.0).then_inc(consts_ready, 1)
            pool.memset(both[:, NB, :], 0.0).then_inc(consts_ready, 1)
            kw = dict(allow_small_or_imprecise_dtypes=True)
            pool.iota(iota_e[:], pattern=[[1, NE]], base=0, channel_multiplier=0, **kw).then_inc(consts_ready, 1)
            pool.iota(iota_t[:], pattern=[[1, NTP]], base=0, channel_multiplier=0, **kw).then_inc(consts_ready, 1)
            pool.iota(iota_r[:], pattern=[[1, P]], base=0, channel_multiplier=0, **kw).then_inc(consts_ready, 1)
            pool.iota(pair_no[:], pattern=[[NTOK, 2], [P, NB]], base=1, channel_multiplier=1, **kw).then_inc(consts_ready, 1)
            pool.iota(limits[:], pattern=[[P, NB]], base=0, channel_multiplier=0, **kw).then_inc(consts_ready, 1)
            pool.iota(pad_row[:], pattern=[[P, NTP]], base=PAIRS + 1, channel_multiplier=1, **kw).then_inc(consts_ready, 1)

            for c in range(NCH):
                pool.wait_ge(exps_ready, c + 1)
                if c >= 2:
                    pool.wait_ge(yw_ready, c - 1)
                pool.tensor_tensor(e2v[:, c % 2], ex[:, c % 2, 2, :, 1:TP], kv[:, c, 1, :, 1:TP],
                                   ALU.mult).then_inc(e2v_ready, 1)
                rsqrt(1, c)

            def gather(i):
                pool.indirect_dma_start(xg[:, i % 4, :], None, xn_rows,
                                        bass.IndirectOffsetOnAxis(token_u[:, i:i + 1], 0)).then_inc(rows_gathered[i % 4], 16)

            def scatter(i):
                pool.wait_ge(yt_ready, i + 1)
                pool.indirect_dma_start(y_rows, bass.IndirectOffsetOnAxis(pair_u[:, i:i + 1], 0),
                                        yt[:, i % 2, :], None).then_inc(rows_scattered[i % 2], 16)

            pool.wait_ge(indices_ready, 2)
            for q in range(4):
                pool.wait_ge(xn_stored[q], 16 * (NB // 4))
            AHEAD = 4
            for i in range(AHEAD):
                gather(i)
            for i in range(NT + 2):
                if i + AHEAD < NT:
                    pool.wait_ge(xg_turned, i + 1)
                    gather(i + AHEAD)
                if i >= 2:
                    scatter(i - 2)

        @block.scalar
        def _(act):
            with nc.allow_non_contiguous_dma(reason="two columns of 128 words"):
                act.dma_start(cols[:, 0, :], decay.rearrange("(c p) -> p c", p=P)).then_inc(small_in, 16)
                act.dma_start(cols[:, 1, :], first.rearrange("(c p) -> p c", p=P)).then_inc(small_in, 16)
            act.dma_start(gates[:, 0:1], g_xattn.rearrange("(a b) -> a b", a=1).to_broadcast([P, 1])).then_inc(small_in, 16)
            act.dma_start(gates[:, 1:2], g_ffn.rearrange("(a b) -> a b", a=1).to_broadcast([P, 1])).then_inc(small_in, 16)
            for c in range(NCH):
                act.dma_start(v_rows[:, 2 * c:2 * c + 2, :], v_dram[:, 2 * c:2 * c + 2, :]).then_inc(v_in[c], 16)
            act.wait_ge(small_in, 16 * 5)
            act.activation(tg[:], gates[:], ACT.Tanh).then_inc(gates_ready, 1)
            act.activation(wcol[:], cols[:, 0, :], ACT.Exp).then_inc(gates_ready, 1)

            def norm_in(b):
                act.wait_ge(shift_ready, b // 2 + 1)
                act.activation(kn[:, b, :], x1[:, b, :], ACT.Identity, bias=shift[:, 0, b:b + 1],
                               scale=rstd[:, 0, b:b + 1]).then_inc(kn_ready, 1)

            def move_kv(b):
                c = b // 2
                act.wait_ge(in_turned, b + 1)
                act.activation(kv[:, c, :, DC * (b % 2):DC * (b % 2) + DC, 1:TP],
                               bank_in[:, b % 2, :].rearrange("p (k s t) -> p k s t", k=2, s=DC),
                               ACT.Copy).then_inc(kv_ready, 1)

            def exps(c):
                act.wait_ge(diff_ready, c + 1)
                if c == 0:
                    act.wait_ge(decay_ready, 3)
                if c >= 2:
                    act.wait_ge(yw_ready, c - 1)
                    act.wait_ge(e2v_ready, c - 1)
                e = ex[:, c % 2]
                n = 0
                for k in range(DC):
                    a = diff[:, c % 2, k:SEQ:DC, :]
                    w, u, neg_w, neg_u = wcol[:, k:k + 1], cols[:, 1, k:k + 1], neg_cols[:, 0, k:k + 1], neg_cols[:, 1, k:k + 1]
                    for kind, (scale, bias) in enumerate(((-1.0, u), (-1.0, neg_w), (1.0, neg_u), (1.0, w))):
                        act.activation(e[:, kind, k:SEQ:DC, 1:TP], a, ACT.Relu, bias=bias,
                                       scale=scale).then_inc(relu_done, 1)
                act.wait_ge(relu_done, 4 * DC * (c + 1))
                flat = e[:, :, :, 1:TP].rearrange("p k s t -> p (k s) t")
                act.activation(flat, flat, ACT.Exp, scale=-1.0).then_inc(exps_ready, 1)

            def move_xnT(c):
                act.wait_ge(xn_turned, c + 1)
                act.activation(xnT[:, 2 * c:2 * c + 2], bank_x[:].rearrange("p (b c t) -> p b c t", b=2, c=DC),
                               ACT.Copy).then_inc(xnT_ready, 1)

            def move_logits(c):
                act.wait_ge(logits_ready, c + 1)
                act.activation(lg[:, 2 * c:2 * c + 2, :],
                               bank_l[:, 2 * c * NE:(2 * c + 2) * NE].rearrange("p (b e) -> p b e", e=NE),
                               ACT.Copy).then_inc(lg_ready, 1)

            def shared_tanh(b):
                act.wait_ge(sgu_ready, b + 1)
                if b >= 2:
                    act.wait_ge(hs_ready, b - 1)
                act.activation(th[:, b % 2], sg_banks[b % 2][:, 0, 0:SJ], ACT.Tanh, scale=0.5).then_inc(sth_ready, 1)

            def move_hsT(b):
                act.wait_ge(hs_turned, b + 1)
                if b >= 2:
                    act.wait_ge(sy_ready, b - 1)
                full = SJ // P
                act.activation(hsT[:, b % 2, 0:full, :], bank_h[:, 0:full * P].rearrange("p (k t) -> p k t", t=P),
                               ACT.Copy).then_inc(hsT_ready, 1)
                rest = SCH[full][1]
                act.activation(hsT[0:rest, b % 2, full, :], bank_h[0:rest, full * P:(full + 1) * P],
                               ACT.Copy).then_inc(hsT_ready, 1)

            def move_gate():
                act.wait_ge(gate_turned, 1)
                act.activation(gate_t[:], bank_h[:, 0:DC * NE].rearrange("p (c e) -> p c e", c=DC),
                               ACT.Copy).then_inc(gate_ready, 1)

            norm_in(0)
            norm_in(1)
            move_kv(0)
            move_kv(1)
            norm_in(2)
            norm_in(3)
            exps(0)
            move_kv(2)
            move_kv(3)
            norm_in(4)
            norm_in(5)
            move_gate()
            exps(1)
            move_kv(4)
            move_kv(5)
            norm_in(6)
            norm_in(7)
            move_kv(6)
            move_kv(7)
            for c in range(NCH):
                if c >= 1:
                    shared_tanh(2 * c - 2)
                    shared_tanh(2 * c - 1)
                    move_hsT(2 * c - 2)
                    move_hsT(2 * c - 1)
                if c + 2 < NCH:
                    exps(c + 2)
                move_xnT(c)
                move_logits(c)
            for b in LAST:
                shared_tanh(b)
            for b in LAST:
                move_hsT(b)
            act.wait_ge(esub_ready, 2)
            act.activation(esub, esub, ACT.Exp).then_inc(eexp_ready, 1)
            act.activation(etop[:], etop[:], ACT.Exp).then_inc(eexp_ready, 1)

            def silu(i, par):
                act.wait_ge(gu_ready, i + 1)
                act.activation(sg[:, par, :], gu_bank[par][:, 0:J], ACT.Silu).then_inc(sg_ready, 1)

            def move_y(i, par, reused):
                act.wait_ge(y_ready, i + 1)
                if reused is not None:
                    act.wait_ge(rows_scattered[par], reused)
                act.activation(yt[:, par, :], yo_bank[par][:, 0:D], ACT.Copy).then_inc(yt_ready, 1)

            for i in range(4):
                silu(i, i % 2)
                if i >= 2:
                    move_y(i - 2, i % 2, None)
            with act.Fori(0, (NT - 5) // 2) as r:
                for u in range(2):
                    silu(2 * r + (4 + u), u)
                    move_y(2 * r + (2 + u), u, 16 * r + 16)
            silu(NT - 1, (NT - 1) % 2)
            for i in range(NT - 3, NT):
                move_y(i, i % 2, 16 * (i // 2))

        @block.tensor
        def _(pe):
            pe.wait_ge(consts_ready, 1)
            pe.wait_ge(small_in, 16 * 5)
            for k in range(DC):
                mm = pe.transpose(bank_h[:, k * NE:(k + 1) * NE], gate_rows[:, k * P:(k + 1) * P], ident[0:NE, 0:NE])
            mm.then_inc(gate_turned, 1)

            def turn_in(b):
                c = b // 2
                pe.wait_ge(kn_ready, b + 1)
                pe.wait_ge(v_in[c], 16)
                if b >= 2:
                    pe.wait_ge(kv_ready, b - 1)
                for s, rows in enumerate((kn, v_rows)):
                    for k in range(DC):
                        at = (s * DC + k) * P
                        mm = pe.transpose(bank_in[:, b % 2, at:at + P], rows[:, b, k * P:(k + 1) * P], ident[:])
                mm.then_inc(in_turned, 1)

            def turn_yw(c):
                pe.wait_ge(yw_ready, c + 1)
                if c >= 2:
                    pe.wait_ge(sy_added, 2 * c - 2)
                for s in range(SEQ):
                    mm = pe.transpose(bank_y[:, s * P:(s + 1) * P], yw[:, c % 2, s, :], ident[:])
                mm.then_inc(yw_turned, 1)

            def turn_xn(c):
                pe.wait_ge(xn_ready, 2 * c + 2)
                for n in range(2):
                    for k in range(DC):
                        at = (DC * n + k) * P
                        mm = pe.transpose(bank_x[:, at:at + P], xn[:, (2 * c + n) % 4, k * P:(k + 1) * P], ident[:])
                mm.then_inc(xn_turned, 1)

            def logits(c):
                pe.wait_ge(xnT_ready, c + 1)
                if c == 0:
                    pe.wait_ge(gate_ready, 1)
                else:
                    pe.wait_ge(lg_ready, c)
                for b in (2 * c, 2 * c + 1):
                    for k in range(DC):
                        mm = pe.matmul(bank_l[:, b * NE:(b + 1) * NE], xnT[:, b, k, :], gate_t[:, k, :],
                                       start=(k == 0), stop=(k == DC - 1))
                mm.then_inc(logits_ready, 1)

            def shared_up(b):
                if b == 0:
                    pe.wait_ge(shared_in, 16 * (1 + len(SCH)))
                if b == 1:
                    pe.wait_ge(kv_ready, NB)
                if b >= 2:
                    pe.wait_ge(hs_ready, b - 1)
                for n in range(2):
                    for k in range(DC):
                        mm = pe.matmul(sg_banks[b % 2][:, n, 0:SJ], xnT[:, b, k, :], s_gu[:, k, n * SJ:(n + 1) * SJ],
                                       start=(k == 0), stop=(k == DC - 1))
                mm.then_inc(sgu_ready, 1)

            def turn_hs(b):
                pe.wait_ge(hs_ready, b + 1)
                if b >= 1:
                    pe.wait_ge(hsT_ready, 2 * b)
                for k, (at, n) in enumerate(SCH):
                    mm = pe.transpose(bank_h[0:n, k * P:(k + 1) * P], hs[:, b % 2, at:at + n], ident[:])
                mm.then_inc(hs_turned, 1)

            def shared_down(b):
                pe.wait_ge(hsT_ready, 2 * b + 2)
                if b < NB - 2:
                    pe.wait_ge(x1_ready, b // 2 + 2)
                if b >= 1:
                    pe.wait_ge(sy_added, b)
                for k, (at, n) in enumerate(SCH):
                    mm = pe.matmul(bank_y[:, 0:D], hsT[0:n, b % 2, k, :], s_dn[0:n, k, :],
                                   start=(k == 0), stop=(k == len(SCH) - 1))
                mm.then_inc(sy_ready, 1)

            for b in range(NB):
                turn_in(b)
            for c in range(NCH):
                if c >= 1:
                    shared_up(2 * c - 2)
                    shared_up(2 * c - 1)
                turn_yw(c)
                if c >= 1:
                    for b in (2 * c - 2, 2 * c - 1):
                        turn_hs(b)
                        shared_down(b)
                turn_xn(c)
                logits(c)
            for b in LAST:
                shared_up(b)

            pe.wait_ge(both_ready, 1)
            pe.wait_ge(consts_ready, 11)
            pe.matmul(bank_l[:, 0:(NB + 1) * NE], tri[:], both[:].rearrange("p b e -> p (b e)"), start=True, stop=False)
            for b in range(NB):
                mm = pe.matmul(bank_l[:, (b + 1) * NE:(NB + 1) * NE].rearrange("p (b e) -> p b e", e=NE), ones[:],
                               both[:, b:b + 1, :].to_broadcast([P, NB - b, NE]), start=False, stop=(b == NB - 1))
            mm.then_inc(ranks_ready, 1)
            turn_hs(LAST[0])
            shared_down(LAST[0])
            turn_hs(LAST[1])
            pe.wait_ge(hot_ready, 1)
            for q in range(2 * NB):
                pe.wait_ge(hot_ready, q + 2)
                mm = pe.matmul(bank_x[:, 0:NTP], row_hot[:, q, :], tile_val[:, q, :], start=(q == 0), stop=(q == 2 * NB - 1))
            mm.then_inc(table_ready, 1)
            shared_down(LAST[1])

            def turn_x(i, par, q4, landed):
                pe.wait_ge(rows_gathered[q4], landed)
                for k in range(DC):
                    mm = pe.transpose(t_bank[par][:, k * P:(k + 1) * P], xg[:, q4, k * P:(k + 1) * P], ident[:])
                mm.then_inc(xg_turned, 1)

            def gate_up(i, par, expert):
                pe.wait_ge(xgT_ready, i + 1)
                for k in range(DC):
                    mm = pe.matmul(gu_bank[par][:, 0:J2], xgT[:, par, k, :],
                                   w_gu[:, bass.ds(expert, 1), k, :].rearrange("p a j -> p (a j)"),
                                   start=(k == 0), stop=(k == DC - 1))
                mm.then_inc(gu_ready, 1)

            def turn_h(i, par):
                pe.wait_ge(h_ready, i + 1)
                for k in range(2):
                    mm = pe.transpose(ht_bank[par][0:JH, k * P:(k + 1) * P], h[:, par, k * JH:(k + 1) * JH], ident[:])
                mm.then_inc(h_turned, 1)

            def down(i, par, expert, reused=True):
                pe.wait_ge(hT_ready, i + 1)
                if reused:
                    pe.wait_ge(yt_ready, i - 1)
                for k in range(2):
                    mm = pe.matmul(yo_bank[par][:, 0:D], hT[:, par, k, :],
                                   w_dn[:, bass.ds(expert, 1), k, :].rearrange("p a d -> p (a d)"),
                                   start=(k == 0), stop=(k == 1))
                mm.then_inc(y_ready, 1)

            def owner_of(i):
                return pe.value_load(owner[0:1, bass.ds(i, 1)], min_val=0, max_val=NE - 1)

            def edge(i):
                if i < NT:
                    gate_up(i, i % 2, owner_of(i))
                if 1 <= i <= NT:
                    turn_h(i - 1, (i - 1) % 2)
                if i + 1 < NT:
                    turn_x(i + 1, (i + 1) % 2, (i + 1) % 4, 16 * ((i + 1) // 4 + 1))
                if i >= 2:
                    down(i - 2, i % 2, owner_of(i - 2), reused=(i >= 4))

            pe.wait_ge(owner_ready, 1)
            pe.wait_ge(experts_in, 16 * 8)
            pe.wait_ge(sy_added, NB)
            turn_x(0, 0, 0, 16)
            for i in range(4):
                edge(i)
            ROUNDS = (NT - 4) // 4
            with pe.Fori(0, ROUNDS) as r:
                owners = []
                for u in range(4):
                    i = 4 * r + (4 + u)
                    owners.append(owner_of(i))
                    gate_up(i, u % 2, owners[u])
                    before = owners[u - 2] if u >= 2 else owner_of(4 * r + (2 + u))
                    turn_h(4 * r + (3 + u), (u + 1) % 2)
                    turn_x(None, (u + 1) % 2, (u + 1) % 4, 16 * r + (32 if u < 3 else 48))
                    down(4 * r + (2 + u), u % 2, before)
            for i in range(4 + 4 * ROUNDS, NT + 2):
                edge(i)

        @block.vector
        def _(dve):
            steps = [0]

            def do(ins):
                steps[0] += 1
                ins.then_inc(dve_step, 1)
                return steps[0]

            def need(n):
                dve.wait_ge(dve_step, n)

            def settle():
                need(steps[0])

            do(dve.memset(kv[:, :, 0, :, 0:1].rearrange("p c s o -> p c (s o)"), NEG))
            do(dve.memset(decay_t[:], 0.0))
            do(dve.memset(ex[:, :, :, :, 0:1].rearrange("p a k s o -> p (a k) (s o)"), 0.0))
            do(dve.memset(vb[:, :, 0:1], 0.0))
            settle()
            do(dve.memset(decay_t[:, :, 0:1], NEG))

            def variance(which, c):
                a = do(dve.bn_stats(stats[:, 2 * c, :], x1[:, 2 * c, :]))
                b = do(dve.bn_stats(stats[:, 2 * c + 1, :], x1[:, 2 * c + 1, :]))
                need(a)
                do(dve.bn_aggr(mv[:, 2 * c, :], stats[:, 2 * c, :]))
                need(b)
                do(dve.bn_aggr(mv[:, 2 * c + 1, :], stats[:, 2 * c + 1, :]))
                settle()
                dve.tensor_scalar(vpe[:, 2 * c:2 * c + 2], mv[:, 2 * c:2 * c + 2, 1], EPS, None,
                                  ALU.add).then_inc(var_ready, 1)

            def shifts(c):
                dve.wait_ge(rstd_ready, c + 1)
                pair = slice(2 * c, 2 * c + 2)
                dve.scalar_tensor_tensor(shift[:, 0, pair], mv[:, pair, 0], -1.0, rstd[:, 0, pair], ALU.mult,
                                         ALU.mult).then_inc(shift_ready, 1)

            def differences(c):
                dve.wait_ge(kv_ready, 2 * c + 2)
                k_all = kv[:, c, 0].rearrange("p s t -> p (s t)")
                n = do(dve.tensor_tensor_scan(pp[:, c % 2].rearrange("p s t -> p (s t)"),
                                              decay_t[:].rearrange("p s t -> p (s t)"), k_all, NEG, ALU.add, ALU.max))
                yield n
                need(n)
                if c >= 2:
                    dve.wait_ge(relu_done, 4 * DC * (c - 1))
                dve.tensor_tensor(diff[:, c % 2], pp[:, c % 2, :, 0:T], kv[:, c, 0, :, 1:TP],
                                  ALU.subtract).then_inc(diff_ready, 1)
                yield

            def recurrence(c, between):
                par = c % 2
                e1, e1b, e2, e2b = (ex[:, par, k] for k in range(4))
                v = kv[:, c, 1, :, 1:TP]
                flat = "p s t -> p (s t)"
                dve.wait_ge(exps_ready, c + 1)
                ev = do(dve.tensor_tensor(vb[:, :, 1:TP], e2b[:, :, 1:TP], v, ALU.mult))
                b = do(dve.tensor_tensor_scan(bb[:].rearrange(flat), e1b.rearrange(flat), e2b.rearrange(flat), 0.0,
                                              ALU.mult, ALU.add))
                need(ev)
                a = do(dve.tensor_tensor_scan(aa[:].rearrange(flat), e1b.rearrange(flat), vb[:].rearrange(flat), 0.0,
                                              ALU.mult, ALU.add))
                need(b)
                d = do(dve.tensor_tensor(den, e1[:, :, 1:TP], bb[:, :, 0:T], ALU.mult))
                need(a)
                m = do(dve.tensor_tensor(num, e1[:, :, 1:TP], aa[:, :, 0:T], ALU.mult))
                need(d)
                d = do(dve.tensor_tensor(den, den, e2[:, :, 1:TP], ALU.add))
                need(m)
                dve.wait_ge(e2v_ready, c + 1)
                do(dve.tensor_tensor(num, num, e2v[:, par], ALU.add))
                need(d)
                r = do(dve.reciprocal(den, den))
                between()
                need(r)
                if c >= 2:
                    dve.wait_ge(yw_turned, c - 1)
                dve.tensor_tensor(yw[:, par], num, den, ALU.mult).then_inc(yw_ready, 1)

            def add_yw(c):
                dve.wait_ge(yw_turned, c + 1)
                rows = x1[:, 2 * c:2 * c + 2, :]
                dve.scalar_tensor_tensor(rows, bank_y[:].rearrange("p (b d) -> p b d", b=2), tg[:, 0:1], rows, ALU.mult,
                                         ALU.add).then_inc(x1_ready, 1)
                dve.wait_ge(x1_ready, c + 1)

            def normalise(b):
                if b % 2 == 0:
                    dve.wait_ge(rstd_ready, NCH + b // 2 + 1)
                if b >= 4:
                    dve.wait_ge(xn_stored[b % 4], 16 * (b // 4))
                    dve.wait_ge(xn_turned, b // 2 - 1)
                dve.tensor_scalar(xn[:, b % 4, :], x1[:, b, :], mv[:, b, 0:1], rstd[:, 1, b:b + 1],
                                  ALU.subtract, ALU.mult).then_inc(xn_ready, 1)

            def shared_h(b):
                par = b % 2
                dve.wait_ge(sth_ready, b + 1)
                if b >= 2:
                    dve.wait_ge(hs_turned, b - 1)
                do(dve.scalar_tensor_tensor(hs[:, par], th[:, par], 1.0, sg_banks[par][:, 0, 0:SJ], ALU.add, ALU.mult))
                settle()
                dve.scalar_tensor_tensor(hs[:, par], sg_banks[par][:, 1, 0:SJ], 0.5, hs[:, par], ALU.mult,
                                         ALU.mult).then_inc(hs_ready, 1)

            def add_shared(b):
                dve.wait_ge(sy_ready, b + 1)
                dve.scalar_tensor_tensor(x1[:, b, :], bank_y[:, 0:D], tg[:, 1:2], x1[:, b, :], ALU.mult,
                                         ALU.add).then_inc(sy_added, 1)

            def choose(c):
                dve.wait_ge(lg_ready, c + 1)
                do(dve.max(top[:, 2 * c, :], lg[:, 2 * c, :]))
                n = do(dve.max(top[:, 2 * c + 1, :], lg[:, 2 * c + 1, :]))
                need(n - 1)
                do(dve.max_index(topi[:, 2 * c, :], top[:, 2 * c, :], lg[:, 2 * c, :]))
                need(n)
                do(dve.max_index(topi[:, 2 * c + 1, :], top[:, 2 * c + 1, :], lg[:, 2 * c + 1, :]))

            def decays():
                dve.wait_ge(gates_ready, 2)
                do(dve.tensor_copy(neg_cols[:, 0], wcol[:]))
                dve.tensor_scalar(neg_cols[:, 1], cols[:, 1], -1.0, None, ALU.mult).then_inc(decay_ready, 1)
                settle()
                dve.tensor_scalar(wcol[:], wcol[:], -1.0, None, ALU.mult).then_inc(decay_ready, 1)
                dve.wait_ge(decay_ready, 2)
                for k in range(DC):
                    at = decay_t[:, k:SEQ:DC, 1:TP]
                    ins = dve.tensor_scalar(at, at, wcol[:, k:k + 1], None, ALU.add)
                    if k == DC - 1:
                        ins.then_inc(decay_ready, 1)
                    else:
                        do(ins)

            def input_variance(c):
                dve.wait_ge(x_in[c], 16)
                variance(0, c)

            input_variance(0)
            input_variance(1)
            decays()
            dve.wait_ge(decay_ready, 3)
            shifts(0)
            shifts(1)
            input_variance(2)
            for _ in differences(0):
                pass
            input_variance(3)
            shifts(2)
            for _ in differences(1):
                pass
            shifts(3)

            for c in range(NCH):
                b0, b1 = 2 * c - 2, 2 * c - 1

                def first_half():
                    if c >= 1:
                        shared_h(b0)

                recurrence(c, first_half)
                if c >= 1:
                    shared_h(b1)
                ahead = differences(c + 2) if c + 2 < NCH else iter(())
                next(ahead, None)
                add_yw(c)
                variance(1, c)
                if c >= 1:
                    choose(c - 1)
                    add_shared(b0)
                next(ahead, None)
                normalise(2 * c)
                normalise(2 * c + 1)
                if c >= 1:
                    add_shared(b1)

            choose(NCH - 1)
            settle()
            dve.wait_ge(consts_ready, 11)
            for k in range(2):
                do(dve.tensor_tensor(mask[:, k], iota_e[:].unsqueeze(1).to_broadcast([P, NB, NE]),
                                     topi[:, :, k:k + 1].to_broadcast([P, NB, NE]), ALU.is_equal))
            settle()
            dve.tensor_tensor(both[:, 0:NB, :], mask[:, 0], mask[:, 1], ALU.add).then_inc(both_ready, 1)
            for b in LAST:
                shared_h(b)
            dve.wait_ge(ranks_ready, 1)
            total = bank_l[:, NB * NE:(NB + 1) * NE]
            do(dve.tensor_tensor(over, total.unsqueeze(2).to_broadcast([P, NE, NB]),
                                 limits[:].unsqueeze(1).to_broadcast([P, NE, NB]), ALU.is_gt))
            settle()
            do(dve.tensor_reduce(tiles[:], over, AX.X, ALU.add))
            settle()
            do(dve.tensor_tensor_scan(ends[:], ones_f[:], tiles[:], 0.0, ALU.mult, ALU.add))
            settle()
            do(dve.tensor_tensor(begins[:], ends[:], tiles[:], ALU.subtract))
            settle()
            do(dve.scalar_tensor_tensor(slot_e, begins[:].unsqueeze(1).to_broadcast([P, NB, NE]), float(P),
                                        bank_l[:, 0:NB * NE].rearrange("p (b e) -> p b e", e=NE), ALU.mult, ALU.add))
            settle()
            for k in range(2):
                do(dve.tensor_tensor(slot_m[:, k], mask[:, k], slot_e, ALU.mult))
            settle()
            do(dve.tensor_reduce(slot[:], slot_m.rearrange("p k b e -> p (k b) e"), AX.X, ALU.add))
            settle()
            do(dve.tensor_copy(slot_u[:], slot[:]))
            settle()
            do(dve.tensor_single_scalar(row_u[:], slot_u[:], P - 1, ALU.bitwise_and))
            do(dve.tensor_single_scalar(tile_u[:], slot_u[:], 7, ALU.logical_shift_right))
            settle()
            do(dve.tensor_copy(row_f[:], row_u[:]))
            do(dve.tensor_tensor(tile_hot, iota_t[:].unsqueeze(1).to_broadcast([P, 2 * NB, NTP]),
                                 tile_u[:].unsqueeze(2).to_broadcast([P, 2 * NB, NTP]), ALU.is_equal))
            settle()
            dve.tensor_tensor(tile_val, tile_hot, pair_no[:].unsqueeze(2).to_broadcast([P, 2 * NB, NTP]),
                              ALU.mult).then_inc(hot_ready, 1)
            for q in range(2 * NB):
                dve.tensor_scalar(row_hot[:, q, :], iota_r[:], row_f[:, q:q + 1], None,
                                  ALU.is_equal).then_inc(hot_ready, 1)
            dve.wait_ge(table_ready, 1)
            do(dve.scalar_tensor_tensor(pad_val[:], bank_x[:, 0:NTP], 0.0, pad_row[:], ALU.is_equal, ALU.mult))
            settle()
            dve.scalar_tensor_tensor(pair_u[:], bank_x[:, 0:NTP], -1.0, pad_val[:], ALU.add,
                                     ALU.add).then_inc(indices_ready, 1)
            dve.wait_ge(indices_ready, 1)
            dve.tensor_single_scalar(token_u[:], pair_u[:], NTOK - 1, ALU.bitwise_and).then_inc(indices_ready, 1)
            do(dve.tensor_tensor(ended, ends[0:1, :].unsqueeze(1).to_broadcast([1, NTP, NE]),
                                 iota_t[0:1, :].unsqueeze(2).to_broadcast([1, NTP, NE]), ALU.is_le))
            settle()
            do(dve.tensor_reduce(owner_f[:], ended, AX.X, ALU.add))
            settle()
            dve.tensor_scalar(owner[:], owner_f[:], float(NE - 1), None, ALU.min).then_inc(owner_ready, 1)
            add_shared(LAST[0])
            dve.tensor_tensor(esub, lg[:], top[:, :, 0:1].to_broadcast([P, NB, NE]),
                              ALU.subtract).then_inc(esub_ready, 1)
            dve.tensor_tensor(etop[:], top[:, :, 1], top[:, :, 0], ALU.subtract).then_inc(esub_ready, 1)
            add_shared(LAST[1])
            dve.wait_ge(eexp_ready, 2)
            do(dve.tensor_reduce(esum[:], esub, AX.X, ALU.add))
            settle()
            do(dve.reciprocal(esum[:], esum[:]))
            settle()
            do(dve.tensor_scalar(wts[:, 0], esum[:], tg[:, 1:2], None, ALU.mult))
            settle()
            do(dve.tensor_tensor(wts[:, 1], wts[:, 0], etop[:], ALU.mult))
            settle()

            def move_x(i, par):
                dve.wait_ge(xg_turned, i + 1)
                dve.tensor_copy(xgT[:, par].rearrange("p c t -> p (c t)"), t_bank[par][:, 0:DC * P]).then_inc(xgT_ready, 1)

            def gated(i, par):
                dve.wait_ge(sg_ready, i + 1)
                dve.tensor_tensor(h[:, par, :], sg[:, par, :], gu_bank[par][:, J:J2], ALU.mult).then_inc(h_ready, 1)

            def move_h(i, par):
                dve.wait_ge(h_turned, i + 1)
                dve.tensor_copy(hT[:, par].rearrange("p c t -> p (c t)"), ht_bank[par][0:JH, 0:2 * P]).then_inc(hT_ready, 1)

            def edge(i):
                if 1 <= i <= NT:
                    move_h(i - 1, (i - 1) % 2)
                if i + 1 < NT:
                    move_x(i + 1, (i + 1) % 2)
                if i < NT:
                    gated(i, i % 2)

            move_x(0, 0)
            edge(0)
            edge(1)
            with dve.Fori(0, (NT - 3) // 2) as r:
                for u in range(2):
                    move_h(2 * r + (1 + u), 1 - u)
                    move_x(2 * r + (3 + u), 1 - u)
                    gated(2 * r + (2 + u), u)
            for i in range(NT - 1, NT + 1):
                edge(i)

            for b in range(NB):
                dve.wait_ge(y_back[b], 16)
                do(dve.scalar_tensor_tensor(x1[:, b, :], y2[:, b, 0, :], wts[:, 0, b:b + 1], x1[:, b, :], ALU.mult,
                                            ALU.add))
                settle()
                dve.scalar_tensor_tensor(x1[:, b, :], y2[:, b, 1, :], wts[:, 1, b:b + 1], x1[:, b, :], ALU.mult,
                                         ALU.add).then_inc(out_ready, 1)


_INS = ['x', 'ctx_2048', 'g_xattn', 'g_ffn', 'L0_xattn_time_decay', 'L0_xattn_time_first', 'L0_ffn_gate_w',
        'L0_ffn_w_gate_up', 'L0_ffn_w_down', 'L0_ffn_shared_gate_up', 'L0_ffn_shared_down']


def kernel(**inputs):
    import numpy as np
    import concourse.bacc as bacc
    from concourse.bass_utils import run_bass_kernel_spmd

    nc = bacc.Bacc("TRN2", target_bir_lowering=False, num_devices=1)
    arrays, args = {}, []
    for name in _INS:
        a = np.ascontiguousarray(inputs[name])
        arrays[f"in_{name}"] = a
        args.append(nc.dram_tensor(f"in_{name}", a.shape, mybir.dt.from_np(a.dtype), kind="ExternalInput").ap())
    out = nc.dram_tensor("out", inputs['x'].shape, F32, kind="ExternalOutput").ap()
    gated_wkv_moe(nc, *args, out)
    r = run_bass_kernel_spmd(nc, [arrays], core_ids=[0])
    return r.results[0]["out"]
```

```python
from contextlib import ExitStack

import concourse.bass as bass
from concourse import mybir

ALU = mybir.AluOpType
ACT = mybir.ActivationFunctionType
AX = mybir.AxisListType
F32 = mybir.dt.float32
F16 = mybir.dt.float16
BF16 = mybir.dt.bfloat16
U32 = mybir.dt.uint32
I32 = mybir.dt.int32

P = 128
EPS = 1e-5
NEG = -1e38


def gated_wkv_moe(nc, x, ctx_in, g_xattn, g_ffn, decay, first, gate_w, w_gate_up, w_down, s_gate_up, s_down, out):
    NB, T, D = x.shape
    NE, _, J2 = w_gate_up.shape
    J = J2 // 2
    S2 = s_gate_up.shape[1]
    SJ = S2 // 2
    NTOK = NB * T
    DC = D // P
    JH = J // 2
    PAIRS = 2 * NTOK
    NT = PAIRS // P + NE - 1
    NTP = 32
    SEQ = 2 * DC
    TP = T + 1
    NCH = NB // 2
    SCH = [(k * P, min(P, SJ - k * P)) for k in range((SJ + P - 1) // P)]
    SW = len(SCH) * P
    assert T == P and DC == 2 and NT < NTP and JH <= P and PAIRS <= 2048

    xn_rows = nc.dram_tensor("xn_rows", (NTOK, D), F32, kind="Internal").ap()
    y_rows = nc.dram_tensor("y_rows", (PAIRS + NT * P, D), F32, kind="Internal").ap()

    with ExitStack() as ctx:
        def sb(name, shape, dt=F32):
            return ctx.enter_context(nc.sbuf_tensor(name, shape, dt))

        def psum(name, shape, dt=F32):
            return ctx.enter_context(nc.psum_tensor(name, shape, dt))

        def sem(name):
            return ctx.enter_context(nc.semaphore(name))

        w_gu = sb("w_gu", [P, NE, DC, J2])
        w_dn = sb("w_dn", [JH, NE, 2, D])
        s_gu = sb("s_gu", [P, DC, SJ + SW])
        s_dn = sb("s_dn", [P, len(SCH), D])
        gate_rows = sb("gate_rows", [NE, D])
        gate_t = sb("gate_t", [P, DC, NE])
        x1 = sb("x1", [P, NB, D])
        xg = sb("xg", [P, NTP, D])
        kn = xg[:, 0:NB, :]
        v_rows = xg[:, NB:2 * NB, :]
        wk = xg[:, 2 * NB:NTP, :].rearrange("p n d -> p (n d)").rearrange("p (q s t) -> p q s t", s=SEQ, t=T)
        yw, e2v, num, den, diff = wk[:, 0:2], wk[:, 2], wk[:, 3], wk[:, 4], wk[:, 5:7]
        y2 = xg[:, 0:2 * NB, :].rearrange("p (b k) d -> p b k d", k=2)
        xn = sb("xn", [P, 4, D])
        stats = sb("stats", [P, NB, 6])
        mv = sb("mv", [P, NB, 2])
        vpe = sb("vpe", [P, NB])
        rstd = sb("rstd", [P, 2, NB])
        neg_half = sb("neg_half", [P, NB])
        first_act = sb("first_act", [P, 1])
        kv = sb("kv", [P, NCH, 2, SEQ, TP])
        pp = sb("pp", [P, 2, SEQ, TP])
        ex = sb("ex", [P, 2, 4, SEQ, TP])
        vb = sb("vb", [P, SEQ, TP])
        aa = sb("aa", [P, SEQ, TP])
        bb = sb("bb", [P, SEQ, TP])
        decay_t = sb("decay_t", [P, SEQ, TP])
        cols = sb("cols", [P, 2, DC])
        wcol = sb("wcol", [P, DC])
        neg_cols = sb("neg_cols", [P, 2, DC])
        shift = sb("shift", [P, 2, NB])
        gates = sb("gates", [P, 2])
        tg = sb("tg", [P, 2])
        xnT = sb("xnT", [P, NB, DC, P])
        th = sb("th", [P, 2, SW])
        hsT = sb("hsT", [P, 2, len(SCH), P])
        lg = sb("lg", [P, NB, NE])
        top = sb("top", [P, NB, 8])
        topi = sb("topi", [P, NB, 8], U32)
        mask = sb("mask", [P, 2, NB, NE], BF16)
        both = sb("both", [P, NB + 1, NE], BF16)
        count_u = sb("count_u", [P, NE], U32)
        tiles_u = sb("tiles_u", [P, NE], U32)
        ends = sb("ends", [P, NE + 1])
        slot_u = sb("slot_u", [P, 2 * NB], U32)
        row_u = sb("row_u", [P, 2 * NB], U32)
        tile_u = sb("tile_u", [P, 2 * NB], U32)
        row_f = sb("row_f", [P, 2 * NB])
        free = ex[:].rearrange("p a k s t -> p (a k s t)")
        hot_words, tile_words = 2 * NB * P // 2, 2 * NB * NTP // 2
        row_hot = free[:, 0:hot_words].bitcast(F16).rearrange("p (q r) -> p q r", r=P)
        tile_hot = free[:, hot_words:hot_words + tile_words].bitcast(F16).rearrange("p (q i) -> p q i", i=NTP)
        tile_val = free[:, hot_words + tile_words:hot_words + 2 * tile_words].bitcast(F16).rearrange("p (q i) -> p q i", i=NTP)
        at = hot_words + 2 * tile_words
        slot_e = free[:, at:at + NB * NE].rearrange("p (b e) -> p b e", e=NE)
        at += NB * NE
        slot_m = free[:, at:at + 2 * NB * NE].rearrange("p (k b e) -> p k b e", k=2, e=NE)
        at += 2 * NB * NE
        ended = free[0:1, at:at + NTP * NE].rearrange("p (i e) -> p i e", e=NE)
        at += NTP * NE
        esub = free[:, at:at + NB * NE].rearrange("p (b e) -> p b e", e=NE)
        pad_val = sb("pad_val", [P, NTP])
        pair_u = sb("pair_u", [P, NTP], U32)
        token_u = sb("token_u", [P, NTP], U32)
        owner_f = sb("owner_f", [1, NTP])
        owner = sb("owner", [1, NTP], I32)
        etop = sb("etop", [P, NB])
        esum = sb("esum", [P, NB])
        wts = sb("wts", [P, 2, NB])
        xgT = sb("xgT", [P, 2, DC, P])
        sg = sb("sg", [P, 2, J])
        h = sb("h", [P, 2, J])
        hT = sb("hT", [JH, 2, 2, P])
        yt = sb("yt", [P, 2, D])
        ident = sb("ident", [P, P])
        tri = sb("tri", [P, P], BF16)
        ones = sb("ones", [P, P], BF16)
        ones_f = sb("ones_f", [P, NE])
        iota_e = sb("iota_e", [P, NE])
        iota_t = sb("iota_t", [P, NTP])
        iota_r = sb("iota_r", [P, P], F16)
        pair_no = sb("pair_no", [P, 2 * NB], F16)
        pad_row = sb("pad_row", [P, NTP])

        bank_in = psum("bank_in", [P, 2, 512])
        bank_y = psum("bank_y", [P, 512])
        bank_x = psum("bank_x", [P, 512])
        bank_l = psum("bank_l", [P, 512])
        bank_g = psum("bank_g", [P, 2, 512])
        bank_h = psum("bank_h", [P, 512])

        x_in = [sem(f"x_in{c}") for c in range(NCH)]
        v_in = [sem(f"v_in{c}") for c in range(NCH)]
        cols_in = sem("cols_in")
        gates_in = sem("gates_in")
        router_in = sem("router_in")
        shared_in = sem("shared_in")
        experts_in = sem("experts_in")
        xn_stored = [sem(f"xn_stored{q}") for q in range(4)]
        rows_gathered = [sem(f"rows_gathered{q}") for q in range(4)]
        rows_scattered = [sem(f"rows_scattered{q}") for q in range(2)]
        y_back = [sem(f"y_back{b}") for b in range(NB)]
        last_back = sem("last_back")
        out_stored = sem("out_stored")
        dve_step = sem("dve_step")
        pool_step = sem("pool_step")
        consts_ready = sem("consts_ready")
        zeros_ready = sem("zeros_ready")
        half_ready = sem("half_ready")
        table_loaded = sem("table_loaded")
        gates_ready = sem("gates_ready")
        w_ready = sem("w_ready")
        decay_ready = sem("decay_ready")
        var_ready = sem("var_ready")
        rstd_ready = sem("rstd_ready")
        kn_ready = sem("kn_ready")
        in_turned = sem("in_turned")
        kv_ready = sem("kv_ready")
        shift_ready = sem("shift_ready")
        xn_shift_ready = sem("xn_shift_ready")
        max_ready = sem("max_ready")
        diff_ready = sem("diff_ready")
        relu_done = sem("relu_done")
        dve_relu_done = sem("dve_relu_done")
        exps_ready = sem("exps_ready")
        outer_exps_ready = sem("outer_exps_ready")
        vb_ready = sem("vb_ready")
        aa_ready = sem("aa_ready")
        num_ready = sem("num_ready")
        yw_ready = sem("yw_ready")
        yw_turned = sem("yw_turned")
        x1_ready = sem("x1_ready")
        xn_ready = sem("xn_ready")
        xn_turned = sem("xn_turned")
        xnT_ready = sem("xnT_ready")
        gate_turned = sem("gate_turned")
        gate_ready = sem("gate_ready")
        logits_ready = sem("logits_ready")
        lg_ready = sem("lg_ready")
        sgu_ready = sem("sgu_ready")
        sth_ready = sem("sth_ready")
        hs_ready = sem("hs_ready")
        sy_ready = sem("sy_ready")
        sy_added = sem("sy_added")
        both_ready = sem("both_ready")
        ranks_ready = sem("ranks_ready")
        tile_hot_ready = sem("tile_hot_ready")
        tile_val_ready = sem("tile_val_ready")
        hot_ready = sem("hot_ready")
        table_ready = sem("table_ready")
        indices_ready = sem("indices_ready")
        owner_ready = sem("owner_ready")
        esub_ready = sem("esub_ready")
        eexp_ready = sem("eexp_ready")
        xg_turned = sem("xg_turned")
        xgT_ready = sem("xgT_ready")
        gu_ready = sem("gu_ready")
        sg_ready = sem("sg_ready")
        h_ready = sem("h_ready")
        h_turned = sem("h_turned")
        hT_ready = sem("hT_ready")
        y_ready = sem("y_ready")
        yt_ready = sem("yt_ready")
        out_ready = sem("out_ready")

        x_dram = x.rearrange("b t d -> t b d")
        v_dram = ctx_in.rearrange("b t d -> t b d")
        out_dram = out.rearrange("b t d -> t b d")
        xn_dram = xn_rows.rearrange("(b t) d -> t b d", t=P)
        y_dram = y_rows[0:PAIRS, :].rearrange("(k b t) d -> t b k d", t=P, k=2)
        wgu_dram = w_gate_up.rearrange("e (c p) j -> p e c j", p=P)
        wdn_dram = w_down.rearrange("e (c p) d -> p e c d", p=JH)
        t_bank = [bank_in[:, 0, :], bank_in[:, 1, :]]
        gu_bank = [bank_g[:, 0, :], bank_g[:, 1, :]]
        ht_bank = [bank_y, bank_x]
        sy_bank = [bank_y, bank_x]
        sg_banks = [bank_g, bank_in]
        yo_bank = [bank_l, bank_h]

        block = ctx.enter_context(nc.Block())

        @block.sync
        def _(sp):
            for c in range(NCH):
                sp.dma_start(x1[:, 2 * c:2 * c + 2, :], x_dram[:, 2 * c:2 * c + 2, :]).then_inc(x_in[c], 16)
            for c in range(1, NCH):
                sp.dma_start(v_rows[:, 2 * c:2 * c + 2, :], v_dram[:, 2 * c:2 * c + 2, :]).then_inc(v_in[c], 16)
            sp.dma_start(gates[:, 0:1], g_xattn.rearrange("(a b) -> a b", a=1).to_broadcast([P, 1])).then_inc(gates_in, 16)
            sp.dma_start(gates[:, 1:2], g_ffn.rearrange("(a b) -> a b", a=1).to_broadcast([P, 1])).then_inc(gates_in, 16)
            sp.dma_start(gate_rows[:], gate_w).then_inc(router_in, 16)
            sp.dma_start(s_gu[:, :, 0:S2], s_gate_up.rearrange("(c p) j -> p c j", p=P)).then_inc(shared_in, 16)
            for k, (at, n) in enumerate(SCH):
                sp.dma_start(s_dn[0:n, k, :], s_down[at:at + n, :]).then_inc(shared_in, 16)
            for q in range(4):
                sp.dma_start(w_gu[:, 4 * q:4 * q + 4], wgu_dram[:, 4 * q:4 * q + 4]).then_inc(experts_in, 16)
                sp.dma_start(w_dn[:, 4 * q:4 * q + 4], wdn_dram[:, 4 * q:4 * q + 4]).then_inc(experts_in, 16)
            for b in range(NB):
                sp.wait_ge(xn_ready, b + 1)
                sp.dma_start(xn_dram[:, b, :], xn[:, b % 4, :]).then_inc(xn_stored[b % 4], 16)
            sp.wait_ge(rows_scattered[0], 16 * ((NT + 1) // 2))
            sp.wait_ge(rows_scattered[1], 16 * (NT // 2))
            sp.wait_ge(xg_turned, NT)
            for b in range(NB - 1):
                sp.dma_start(y2[:, b], y_dram[:, b]).then_inc(y_back[b], 16)
            sp.dma_start(y2[:, NB - 1, 0], y_dram[:, NB - 1, 0]).then_inc(y_back[NB - 1], 16)
            sp.dma_start(y2[:, NB - 1, 1], y_dram[:, NB - 1, 1]).then_inc(last_back, 16)
            for b in range(NB):
                sp.wait_ge(out_ready, b + 1)
                sp.dma_start(out_dram[:, b, :], x1[:, b, :]).then_inc(out_stored, 16)
            sp.wait_ge(out_stored, 16 * NB)

        @block.gpsimd
        def _(pool):
            steps = [0]

            def do(ins):
                steps[0] += 1
                ins.then_inc(pool_step, 1)

            def settle():
                pool.wait_ge(pool_step, steps[0])

            do(pool.memset(ident[:], 0.0))
            do(pool.memset(tri[:], 1.0))
            settle()
            pool.affine_select(out=ident[:], in_=ident[:], compare_op=ALU.not_equal, fill=1.0, base=0,
                               pattern=[[-1, P]], channel_multiplier=1).then_inc(consts_ready, 1)
            pool.memset(neg_half[:], -0.5).then_inc(half_ready, 1)
            pool.wait_ge(half_ready, 1)

            def rsqrt(which, c):
                pool.wait_ge(var_ready, NCH * which + c + 1)
                pair = slice(2 * c, 2 * c + 2)
                pool.tensor_tensor(rstd[:, which, pair], vpe[:, pair], neg_half[:, pair],
                                   ALU.pow).then_inc(rstd_ready, 1)

            pool.memset(s_gu[:, :, S2:], 0.0).then_inc(zeros_ready, 1)
            for c in range(NCH):
                rsqrt(0, c)
            pool.affine_select(out=tri[:], in_=tri[:], compare_op=ALU.is_gt, fill=0.0, base=0,
                               pattern=[[1, P]], channel_multiplier=-1).then_inc(consts_ready, 1)
            pool.memset(ones[:], 1.0).then_inc(consts_ready, 1)
            pool.memset(ones_f[:], 1.0).then_inc(consts_ready, 1)
            pool.memset(both[:, NB, :], 0.0).then_inc(consts_ready, 1)
            kw = dict(allow_small_or_imprecise_dtypes=True)
            pool.iota(iota_e[:], pattern=[[1, NE]], base=0, channel_multiplier=0, **kw).then_inc(consts_ready, 1)
            pool.iota(iota_t[:], pattern=[[1, NTP]], base=0, channel_multiplier=0, **kw).then_inc(consts_ready, 1)
            pool.iota(iota_r[:], pattern=[[1, P]], base=0, channel_multiplier=0, **kw).then_inc(consts_ready, 1)
            pool.iota(pair_no[:], pattern=[[NTOK, 2], [P, NB]], base=1, channel_multiplier=1, **kw).then_inc(consts_ready, 1)
            pool.iota(pad_row[:], pattern=[[P, NTP]], base=PAIRS + 1, channel_multiplier=1, **kw).then_inc(consts_ready, 1)

            def pool_difference(c):
                pool.wait_ge(max_ready, c + 1)
                if c >= 2:
                    pool.wait_ge(outer_exps_ready, c - 1)
                pool.tensor_tensor(diff[:, c % 2], pp[:, c % 2, :, 0:T], kv[:, c, 0, :, 1:TP],
                                   ALU.subtract).then_inc(diff_ready, 1)

            for c in range(NCH):
                _, e2b, e1, e2 = (ex[:, c % 2, k, :, 1:TP] for k in range(4))
                v = kv[:, c, 1, :, 1:TP]
                pool.wait_ge(exps_ready, c + 1)
                if c >= 1:
                    pool.wait_ge(aa_ready, c)
                pool.tensor_tensor(vb[:, :, 1:TP], e2b, v, ALU.mult).then_inc(vb_ready, 1)
                pool.wait_ge(outer_exps_ready, c + 1)
                do(pool.tensor_tensor(e2v, e2, v, ALU.mult))
                if c == 0:
                    pool_difference(1)
                pool.wait_ge(aa_ready, c + 1)
                if c >= 1:
                    pool.wait_ge(yw_ready, c)
                do(pool.tensor_tensor(num, e1, aa[:, :, 0:T], ALU.mult))
                settle()
                pool.tensor_tensor(num, num, e2v, ALU.add).then_inc(num_ready, 1)
                if c + 2 < NCH:
                    pool_difference(c + 2)
                rsqrt(1, c)

            pool.wait_ge(tile_hot_ready, 1)
            pool.tensor_tensor(tile_val, tile_hot, pair_no[:].unsqueeze(2).to_broadcast([P, 2 * NB, NTP]),
                               ALU.mult).then_inc(tile_val_ready, 1)

            def gather(i):
                pool.indirect_dma_start(xg[:, i % 4, :], None, xn_rows,
                                        bass.IndirectOffsetOnAxis(token_u[:, i:i + 1], 0)).then_inc(rows_gathered[i % 4], 16)

            def scatter(i):
                pool.wait_ge(yt_ready, i + 1)
                pool.indirect_dma_start(y_rows, bass.IndirectOffsetOnAxis(pair_u[:, i:i + 1], 0),
                                        yt[:, i % 2, :], None).then_inc(rows_scattered[i % 2], 16)

            pool.wait_ge(indices_ready, 2)
            for q in range(4):
                pool.wait_ge(xn_stored[q], 16 * (NB // 4))
            AHEAD = 4
            for i in range(AHEAD):
                gather(i)
            for i in range(NT + 2):
                if i + AHEAD < NT:
                    pool.wait_ge(xg_turned, i + 1)
                    gather(i + AHEAD)
                if i >= 2:
                    scatter(i - 2)

        @block.scalar
        def _(act):
            with nc.allow_non_contiguous_dma(reason="two columns of 128 words"):
                act.dma_start(cols[:, 0, :], decay.rearrange("(c p) -> p c", p=P)).then_inc(cols_in, 16)
                act.dma_start(cols[:, 1, :], first.rearrange("(c p) -> p c", p=P)).then_inc(cols_in, 16)
            act.dma_start(v_rows[:, 0:2, :], v_dram[:, 0:2, :]).then_inc(v_in[0], 16)
            act.wait_ge(half_ready, 1)
            act.activation(first_act[:], neg_half[:, 0:1], ACT.Tanh).then_inc(table_loaded, 1)

            def exp_decay():
                act.wait_ge(cols_in, 32)
                act.activation(wcol[:], cols[:, 0, :], ACT.Exp).then_inc(w_ready, 1)

            def tanh_gates():
                act.wait_ge(gates_in, 32)
                act.activation(tg[:], gates[:], ACT.Tanh).then_inc(gates_ready, 1)

            def norm_in(b):
                act.wait_ge(shift_ready, b // 2 + 1)
                act.activation(kn[:, b, :], x1[:, b, :], ACT.Identity, bias=shift[:, 0, b:b + 1],
                               scale=rstd[:, 0, b:b + 1]).then_inc(kn_ready, 1)

            def move_kv(b):
                c = b // 2
                act.wait_ge(in_turned, b + 1)
                act.activation(kv[:, c, :, DC * (b % 2):DC * (b % 2) + DC, 1:TP],
                               bank_in[:, b % 2, :].rearrange("p (k s t) -> p k s t", k=2, s=DC),
                               ACT.Copy).then_inc(kv_ready, 1)

            def exps_in_parts(c):
                act.wait_ge(diff_ready, c + 1)
                if c == 0:
                    act.wait_ge(decay_ready, 3)
                if c >= 2:
                    act.wait_ge(yw_ready, c - 1)
                    act.wait_ge(num_ready, c - 1)
                relus = 4 * DC * c - (2 * DC if c else 0)
                for half in range(2):
                    for k in range(DC):
                        a = diff[:, c % 2, k:SEQ:DC, :]
                        w, u, neg_w, neg_u = (wcol[:, k:k + 1], cols[:, 1, k:k + 1], neg_cols[:, 0, k:k + 1],
                                              neg_cols[:, 1, k:k + 1])
                        args = ((-1.0, neg_w), (1.0, w)) if half == 0 else ((-1.0, u), (1.0, neg_u))
                        for n, (scale, bias) in enumerate(args):
                            if c == 0 and n == 1:
                                continue
                            act.activation(ex[:, c % 2, 2 * half + n, k:SEQ:DC, 1:TP], a, ACT.Relu, bias=bias,
                                           scale=scale).then_inc(relu_done, 1)
                            relus += 1
                    yield
                    act.wait_ge(relu_done, relus)
                    if c == 0:
                        act.wait_ge(dve_relu_done, DC * (half + 1))
                    e = ex[:, c % 2, 2 * half:2 * half + 2, :, 1:TP].rearrange("p k s t -> p (k s) t")
                    act.activation(e, e, ACT.Exp, scale=-1.0).then_inc(outer_exps_ready if half else exps_ready, 1)

            def exps(c):
                for _ in exps_in_parts(c):
                    pass

            def norm_xn(b):
                act.wait_ge(xn_shift_ready, b // 2 + 1)
                if b >= 4:
                    act.wait_ge(xn_stored[b % 4], 16 * (b // 4))
                    act.wait_ge(xn_turned, b // 2 - 1)
                act.activation(xn[:, b % 4, :], x1[:, b, :], ACT.Identity, bias=shift[:, 1, b:b + 1],
                               scale=rstd[:, 1, b:b + 1]).then_inc(xn_ready, 1)

            def move_xnT(c):
                act.wait_ge(xn_turned, c + 1)
                act.activation(xnT[:, 2 * c:2 * c + 2], bank_x[:].rearrange("p (b c t) -> p b c t", b=2, c=DC),
                               ACT.Copy).then_inc(xnT_ready, 1)

            def move_logits(c):
                act.wait_ge(logits_ready, c + 1)
                act.activation(lg[:, 2 * c:2 * c + 2, :],
                               bank_l[:, 2 * c * NE:(2 * c + 2) * NE].rearrange("p (b e) -> p b e", e=NE),
                               ACT.Copy).then_inc(lg_ready, 1)

            def shared_tanh(b):
                act.wait_ge(sgu_ready, b + 1)
                if b >= 2:
                    act.wait_ge(hs_ready, b - 1)
                act.activation(th[:, b % 2], sg_banks[b % 2][:, 0, 0:SW], ACT.Tanh, scale=0.5).then_inc(sth_ready, 1)

            def move_gate():
                act.wait_ge(gate_turned, 1)
                act.activation(gate_t[:], bank_h[:, 0:DC * NE].rearrange("p (c e) -> p c e", c=DC),
                               ACT.Copy).then_inc(gate_ready, 1)

            exp_decay()
            norm_in(0)
            norm_in(1)
            move_kv(0)
            move_kv(1)
            norm_in(2)
            norm_in(3)
            exps(0)
            move_kv(2)
            move_kv(3)
            tanh_gates()
            norm_in(4)
            norm_in(5)
            move_gate()
            norm_in(6)
            norm_in(7)
            move_kv(4)
            move_kv(5)
            exps(1)
            move_kv(6)
            move_kv(7)
            for c in range(1, NCH + 1):
                ahead = exps_in_parts(c + 1) if c + 1 < NCH else iter(())
                if c < NCH:
                    norm_xn(2 * c - 2)
                    norm_xn(2 * c - 1)
                if c >= 2:
                    shared_tanh(2 * c - 3)
                move_xnT(c - 1)
                next(ahead, None)
                move_logits(c - 1)
                next(ahead, None)
                if c == 1:
                    next(ahead, None)
                shared_tanh(2 * c - 2)
                next(ahead, None)
            act.wait_ge(table_loaded, 1)
            act.activation(first_act[:], neg_half[:, 0:1], ACT.Silu).then_inc(table_loaded, 1)
            shared_tanh(NB - 1)

            def silu(i, par):
                act.wait_ge(gu_ready, i + 1)
                act.activation(sg[:, par, :], gu_bank[par][:, 0:J], ACT.Silu).then_inc(sg_ready, 1)

            def move_y(i, par, reused):
                act.wait_ge(y_ready, i + 1)
                if reused is not None:
                    act.wait_ge(rows_scattered[par], reused)
                act.activation(yt[:, par, :], yo_bank[par][:, 0:D], ACT.Copy).then_inc(yt_ready, 1)

            for i in range(4):
                silu(i, i % 2)
                if i >= 2:
                    move_y(i - 2, i % 2, None)
            with act.Fori(0, (NT - 5) // 2) as r:
                for u in range(2):
                    silu(2 * r + (4 + u), u)
                    move_y(2 * r + (2 + u), u, 16 * r + 16)
            silu(NT - 1, (NT - 1) % 2)
            for i in range(NT - 3, NT):
                move_y(i, i % 2, 16 * (i // 2))
            act.wait_ge(esub_ready, 2)
            act.activation(esub, esub, ACT.Exp).then_inc(eexp_ready, 1)
            act.activation(etop[:], etop[:], ACT.Exp).then_inc(eexp_ready, 1)

        @block.tensor
        def _(pe):
            pe.wait_ge(consts_ready, 1)
            def turn_in(b):
                c = b // 2
                pe.wait_ge(kn_ready, b + 1)
                pe.wait_ge(v_in[c], 16)
                if b >= 2:
                    pe.wait_ge(kv_ready, b - 1)
                for s, rows in enumerate((kn, v_rows)):
                    for k in range(DC):
                        at = (s * DC + k) * P
                        mm = pe.transpose(bank_in[:, b % 2, at:at + P], rows[:, b, k * P:(k + 1) * P], ident[:])
                mm.then_inc(in_turned, 1)

            def turn_yw(c):
                pe.wait_ge(yw_ready, c + 1)
                if c >= 2:
                    pe.wait_ge(sy_added, 2 * c - 3)
                for s in range(SEQ):
                    mm = pe.transpose(bank_y[:, s * P:(s + 1) * P], yw[:, c % 2, s, :], ident[:])
                mm.then_inc(yw_turned, 1)

            def turn_xn(c):
                pe.wait_ge(xn_ready, 2 * c + 2)
                if c >= 2:
                    pe.wait_ge(sy_added, 2 * c - 2)
                for n in range(2):
                    for k in range(DC):
                        at = (DC * n + k) * P
                        mm = pe.transpose(bank_x[:, at:at + P], xn[:, (2 * c + n) % 4, k * P:(k + 1) * P], ident[:])
                mm.then_inc(xn_turned, 1)

            def logits(c):
                pe.wait_ge(xnT_ready, c + 1)
                if c == 0:
                    pe.wait_ge(gate_ready, 1)
                else:
                    pe.wait_ge(lg_ready, c)
                for b in (2 * c, 2 * c + 1):
                    for k in range(DC):
                        mm = pe.matmul(bank_l[:, b * NE:(b + 1) * NE], xnT[:, b, k, :], gate_t[:, k, :],
                                       start=(k == 0), stop=(k == DC - 1))
                mm.then_inc(logits_ready, 1)

            def shared_up(b):
                if b == 0:
                    pe.wait_ge(shared_in, 16 * (1 + len(SCH)))
                    pe.wait_ge(zeros_ready, 1)
                if b == 1:
                    pe.wait_ge(kv_ready, NB)
                if b >= 2:
                    pe.wait_ge(hs_ready, b - 1)
                for n in range(2):
                    for at, _ in SCH:
                        for k in range(DC):
                            mm = pe.matmul(sg_banks[b % 2][:, n, at:at + P], s_gu[:, k, n * SJ + at:n * SJ + at + P],
                                           xnT[:, b, k, :], start=(k == 0), stop=(k == DC - 1))
                mm.then_inc(sgu_ready, 1)

            def shared_down(b):
                pe.wait_ge(hs_ready, b + 1)
                if b % 2 == 0 and b < NB - 2:
                    pe.wait_ge(x1_ready, b // 2 + 2)
                elif b % 2 == 1:
                    pe.wait_ge(xnT_ready, min(b // 2 + 2, NCH))
                if b >= 2:
                    pe.wait_ge(sy_added, b - 1)
                for k, (at, n) in enumerate(SCH):
                    mm = pe.matmul(sy_bank[b % 2][:, 0:D], hsT[0:n, b % 2, k, :], s_dn[0:n, k, :],
                                   start=(k == 0), stop=(k == len(SCH) - 1))
                mm.then_inc(sy_ready, 1)

            def keep_warm(n):
                for _ in range(n):
                    pe.matmul(bank_g[:, 0, 0:D], ident[:], kn[:, 0, :], start=True, stop=True)

            for b in range(2):
                turn_in(b)
            pe.wait_ge(router_in, 16)
            for k in range(DC):
                mm = pe.transpose(bank_h[:, k * NE:(k + 1) * NE], gate_rows[:, k * P:(k + 1) * P], ident[0:NE, 0:NE])
            mm.then_inc(gate_turned, 1)
            for b in range(2, NB):
                turn_in(b)

            for c in range(NCH):
                if c == 1:
                    keep_warm(6)
                if c >= 1:
                    turn_xn(c - 1)
                if c == 1:
                    keep_warm(1)
                if c >= 2:
                    shared_down(2 * c - 4)
                if c >= 1:
                    logits(c - 1)
                if c >= 2:
                    shared_up(2 * c - 2)
                if c == 1:
                    keep_warm(3)
                turn_yw(c)
                if c >= 2:
                    shared_down(2 * c - 3)
                    shared_up(2 * c - 1)
                if c == 1:
                    shared_up(0)
                    shared_up(1)
            turn_xn(NCH - 1)
            logits(NCH - 1)
            shared_down(NB - 4)

            pe.wait_ge(both_ready, 1)
            pe.wait_ge(consts_ready, 10)
            pe.matmul(bank_l[:, 0:(NB + 1) * NE], tri[:], both[:].rearrange("p b e -> p (b e)"), start=True, stop=False)
            for b in range(NB):
                mm = pe.matmul(bank_l[:, (b + 1) * NE:(NB + 1) * NE].rearrange("p (b e) -> p b e", e=NE), ones[:],
                               both[:, b:b + 1, :].to_broadcast([P, NB - b, NE]), start=False, stop=(b == NB - 1))
            mm.then_inc(ranks_ready, 1)
            shared_up(NB - 2)
            shared_up(NB - 1)
            pe.wait_ge(tile_val_ready, 1)
            for q in range(2 * NB):
                pe.wait_ge(hot_ready, q + 1)
                mm = pe.matmul(bank_l[:, 0:NTP], row_hot[:, q, :], tile_val[:, q, :], start=(q == 0), stop=(q == 2 * NB - 1))
            mm.then_inc(table_ready, 1)
            shared_down(NB - 3)
            shared_down(NB - 2)
            shared_down(NB - 1)

            def turn_x(i, par, q4, landed):
                pe.wait_ge(rows_gathered[q4], landed)
                for k in range(DC):
                    mm = pe.transpose(t_bank[par][:, k * P:(k + 1) * P], xg[:, q4, k * P:(k + 1) * P], ident[:])
                mm.then_inc(xg_turned, 1)

            def gate_up(i, par, expert):
                pe.wait_ge(xgT_ready, i + 1)
                for k in range(DC):
                    mm = pe.matmul(gu_bank[par][:, 0:J2], xgT[:, par, k, :],
                                   w_gu[:, bass.ds(expert, 1), k, :].rearrange("p a j -> p (a j)"),
                                   start=(k == 0), stop=(k == DC - 1))
                mm.then_inc(gu_ready, 1)

            def turn_h(i, par):
                pe.wait_ge(h_ready, i + 1)
                for k in range(2):
                    mm = pe.transpose(ht_bank[par][0:JH, k * P:(k + 1) * P], h[:, par, k * JH:(k + 1) * JH], ident[:])
                mm.then_inc(h_turned, 1)

            def down(i, par, expert, reused=True):
                pe.wait_ge(hT_ready, i + 1)
                if reused:
                    pe.wait_ge(yt_ready, i - 1)
                for k in range(2):
                    mm = pe.matmul(yo_bank[par][:, 0:D], hT[:, par, k, :],
                                   w_dn[:, bass.ds(expert, 1), k, :].rearrange("p a d -> p (a d)"),
                                   start=(k == 0), stop=(k == 1))
                mm.then_inc(y_ready, 1)

            def owner_of(i):
                return pe.value_load(owner[0:1, bass.ds(i, 1)], min_val=0, max_val=NE - 1)

            def edge(i):
                if i < NT:
                    gate_up(i, i % 2, owner_of(i))
                if i + 2 < NT:
                    turn_x(i + 2, i % 2, (i + 2) % 4, 16 * ((i + 2) // 4 + 1))
                if 1 <= i <= NT:
                    turn_h(i - 1, (i - 1) % 2)
                if i >= 2:
                    down(i - 2, i % 2, owner_of(i - 2), reused=(i >= 4))

            turn_x(0, 0, 0, 16)
            turn_x(1, 1, 1, 16)
            pe.wait_ge(owner_ready, 1)
            pe.wait_ge(experts_in, 16 * 8)
            edge(0)
            pe.wait_ge(sy_added, NB)
            for i in range(1, 4):
                edge(i)
            ROUNDS = (NT - 4) // 4
            with pe.Fori(0, ROUNDS) as r:
                owners = []
                for u in range(4):
                    i = 4 * r + (4 + u)
                    owners.append(owner_of(i))
                    gate_up(i, u % 2, owners[u])
                    owner_behind = owners[u - 2] if u >= 2 else owner_of(4 * r + (2 + u))
                    turn_x(None, u % 2, (u + 2) % 4, 16 * r + (32 if u < 2 else 48))
                    turn_h(4 * r + (3 + u), (u + 1) % 2)
                    down(4 * r + (2 + u), u % 2, owner_behind)
            for i in range(4 + 4 * ROUNDS, NT + 2):
                edge(i)

        @block.vector
        def _(dve):
            steps = [0]

            def do(ins):
                steps[0] += 1
                ins.then_inc(dve_step, 1)
                return steps[0]

            def need(n):
                dve.wait_ge(dve_step, n)

            def settle():
                need(steps[0])

            do(dve.memset(kv[:, :, 0, :, 0:1].rearrange("p c s o -> p c (s o)"), NEG))
            do(dve.memset(decay_t[:], 0.0))
            do(dve.memset(ex[:, :, :, :, 0:1].rearrange("p a k s o -> p (a k) (s o)"), 0.0))
            do(dve.memset(vb[:, :, 0:1], 0.0))
            do(dve.memset(ends[:, 0:1], 0.0))
            settle()
            do(dve.memset(decay_t[:, :, 0:1], NEG))

            def variance(which, c):
                a = do(dve.bn_stats(stats[:, 2 * c, :], x1[:, 2 * c, :]))
                b = do(dve.bn_stats(stats[:, 2 * c + 1, :], x1[:, 2 * c + 1, :]))
                need(a)
                do(dve.bn_aggr(mv[:, 2 * c, :], stats[:, 2 * c, :]))
                need(b)
                do(dve.bn_aggr(mv[:, 2 * c + 1, :], stats[:, 2 * c + 1, :]))
                settle()
                dve.tensor_scalar(vpe[:, 2 * c:2 * c + 2], mv[:, 2 * c:2 * c + 2, 1], EPS, None,
                                  ALU.add).then_inc(var_ready, 1)

            def shifts(c):
                dve.wait_ge(rstd_ready, c + 1)
                pair = slice(2 * c, 2 * c + 2)
                dve.scalar_tensor_tensor(shift[:, 0, pair], mv[:, pair, 0], -1.0, rstd[:, 0, pair], ALU.mult,
                                         ALU.mult).then_inc(shift_ready, 1)

            def running_max(c):
                dve.wait_ge(kv_ready, 2 * c + 2)
                dve.tensor_tensor_scan(pp[:, c % 2].rearrange("p s t -> p (s t)"),
                                       decay_t[:].rearrange("p s t -> p (s t)"),
                                       kv[:, c, 0].rearrange("p s t -> p (s t)"), NEG, ALU.add,
                                       ALU.max).then_inc(max_ready, 1)

            def first_difference():
                dve.wait_ge(max_ready, 1)
                dve.tensor_tensor(diff[:, 0], pp[:, 0, :, 0:T], kv[:, 0, 0, :, 1:TP],
                                  ALU.subtract).then_inc(diff_ready, 1)
                dve.wait_ge(diff_ready, 1)
                for k in range(DC):
                    dve.tensor_scalar(ex[:, 0, 1, k:SEQ:DC, 1:TP], diff[:, 0, k:SEQ:DC, :], wcol[:, k:k + 1], 0.0,
                                      ALU.add, ALU.max).then_inc(dve_relu_done, 1)
                for k in range(DC):
                    dve.tensor_scalar(ex[:, 0, 3, k:SEQ:DC, 1:TP], diff[:, 0, k:SEQ:DC, :], cols[:, 1, k:k + 1], 0.0,
                                      ALU.subtract, ALU.max).then_inc(dve_relu_done, 1)

            def recurrence(c, after_sum, before_den, after_den):
                par = c % 2
                e1b, e2b, e1, e2 = (ex[:, par, k] for k in range(4))
                flat = "p s t -> p (s t)"
                dve.wait_ge(exps_ready, c + 1)
                b = do(dve.tensor_tensor_scan(bb[:].rearrange(flat), e1b.rearrange(flat), e2b.rearrange(flat), 0.0,
                                              ALU.mult, ALU.add))
                after_sum()
                need(b)
                dve.wait_ge(outer_exps_ready, c + 1)
                d = do(dve.tensor_tensor(den, e1[:, :, 1:TP], bb[:, :, 0:T], ALU.mult))
                dve.wait_ge(vb_ready, c + 1)
                dve.tensor_tensor_scan(aa[:].rearrange(flat), e1b.rearrange(flat), vb[:].rearrange(flat), 0.0,
                                       ALU.mult, ALU.add).then_inc(aa_ready, 1)
                before_den()
                need(d)
                n = do(dve.tensor_tensor(den, den, e2[:, :, 1:TP], ALU.add))
                if c == 2:
                    shared_h(0)
                need(n)
                r = do(dve.reciprocal(den, den))
                after_den()
                need(r)
                dve.wait_ge(num_ready, c + 1)
                if c >= 2:
                    dve.wait_ge(yw_turned, c - 1)
                dve.tensor_tensor(yw[:, par], num, den, ALU.mult).then_inc(yw_ready, 1)

            def add_yw(c):
                dve.wait_ge(yw_turned, c + 1)
                rows = x1[:, 2 * c:2 * c + 2, :]
                dve.scalar_tensor_tensor(rows, bank_y[:].rearrange("p (b d) -> p b d", b=2), tg[:, 0:1], rows, ALU.mult,
                                         ALU.add).then_inc(x1_ready, 1)
                dve.wait_ge(x1_ready, c + 1)

            def shift_xn(c):
                dve.wait_ge(rstd_ready, NCH + c + 1)
                pair = slice(2 * c, 2 * c + 2)
                dve.scalar_tensor_tensor(shift[:, 1, pair], mv[:, pair, 0], -1.0, rstd[:, 1, pair], ALU.mult,
                                         ALU.mult).then_inc(xn_shift_ready, 1)

            def shared_h(b):
                par = b % 2
                dve.wait_ge(sth_ready, b + 1)
                if b >= 2:
                    dve.wait_ge(sy_ready, b - 1)
                hidden = hsT[:, par].rearrange("p c t -> p (c t)")
                do(dve.scalar_tensor_tensor(hidden, th[:, par], 1.0, sg_banks[par][:, 0, 0:SW], ALU.add, ALU.mult))
                settle()
                dve.scalar_tensor_tensor(hidden, sg_banks[par][:, 1, 0:SW], 0.5, hidden, ALU.mult,
                                         ALU.mult).then_inc(hs_ready, 1)

            def add_shared(b):
                dve.wait_ge(sy_ready, b + 1)
                dve.scalar_tensor_tensor(x1[:, b, :], sy_bank[b % 2][:, 0:D], tg[:, 1:2], x1[:, b, :], ALU.mult,
                                         ALU.add).then_inc(sy_added, 1)

            def norm_last_xn():
                dve.wait_ge(rstd_ready, 2 * NCH)
                for b in (NB - 2, NB - 1):
                    dve.wait_ge(xn_stored[b % 4], 16 * (b // 4))
                    dve.wait_ge(xn_turned, b // 2 - 1)
                    dve.tensor_scalar(xn[:, b % 4, :], x1[:, b, :], mv[:, b, 0:1], rstd[:, 1, b:b + 1], ALU.subtract,
                                      ALU.mult).then_inc(xn_ready, 1)

            def choose(c):
                dve.wait_ge(lg_ready, c + 1)
                do(dve.max(top[:, 2 * c, :], lg[:, 2 * c, :]))
                n = do(dve.max(top[:, 2 * c + 1, :], lg[:, 2 * c + 1, :]))
                need(n - 1)
                do(dve.max_index(topi[:, 2 * c, :], top[:, 2 * c, :], lg[:, 2 * c, :]))
                need(n)
                do(dve.max_index(topi[:, 2 * c + 1, :], top[:, 2 * c + 1, :], lg[:, 2 * c + 1, :]))

            def decays():
                dve.wait_ge(w_ready, 1)
                do(dve.tensor_copy(neg_cols[:, 0], wcol[:]))
                dve.tensor_scalar(neg_cols[:, 1], cols[:, 1], -1.0, None, ALU.mult).then_inc(decay_ready, 1)
                settle()
                dve.tensor_scalar(wcol[:], wcol[:], -1.0, None, ALU.mult).then_inc(decay_ready, 1)
                dve.wait_ge(decay_ready, 2)
                for k in range(DC):
                    at = decay_t[:, k:SEQ:DC, 1:TP]
                    ins = dve.tensor_scalar(at, at, wcol[:, k:k + 1], None, ALU.add)
                    if k == DC - 1:
                        ins.then_inc(decay_ready, 1)
                    else:
                        do(ins)

            def input_variance(c):
                dve.wait_ge(x_in[c], 16)
                variance(0, c)

            input_variance(0)
            input_variance(1)
            shifts(0)
            decays()
            shifts(1)
            input_variance(2)
            input_variance(3)
            shifts(2)
            dve.wait_ge(decay_ready, 3)
            running_max(0)
            first_difference()
            shifts(3)

            for c in range(NCH):
                def after_sum():
                    if c >= 1:
                        shift_xn(c - 1)

                def before_den():
                    if c == 0:
                        running_max(1)
                        dve.wait_ge(gates_ready, 1)

                def after_den():
                    if c >= 2:
                        shared_h(2 * c - 3)
                        add_shared(2 * c - 4)

                recurrence(c, after_sum, before_den, after_den)
                if c + 2 < NCH:
                    running_max(c + 2)
                if c >= 2:
                    shared_h(2 * c - 2)
                add_yw(c)
                variance(1, c)
                if c >= 2:
                    add_shared(2 * c - 3)
                if c >= 1:
                    choose(c - 1)
            norm_last_xn()
            shared_h(NB - 3)
            choose(NCH - 1)
            settle()
            dve.wait_ge(consts_ready, 10)
            for k in range(2):
                do(dve.tensor_tensor(mask[:, k], iota_e[:].unsqueeze(1).to_broadcast([P, NB, NE]),
                                     topi[:, :, k:k + 1].to_broadcast([P, NB, NE]), ALU.is_equal))
            settle()
            dve.tensor_tensor(both[:, 0:NB, :], mask[:, 0], mask[:, 1], ALU.add).then_inc(both_ready, 1)
            add_shared(NB - 4)
            dve.wait_ge(ranks_ready, 1)
            total = bank_l[:, NB * NE:(NB + 1) * NE]
            do(dve.tensor_scalar(count_u[:], total, float(P - 1), None, ALU.add))
            settle()
            do(dve.tensor_single_scalar(tiles_u[:], count_u[:], 7, ALU.logical_shift_right))
            settle()
            do(dve.tensor_tensor_scan(ends[:, 1:NE + 1], ones_f[:], tiles_u[:], 0.0, ALU.mult, ALU.add))
            settle()
            do(dve.scalar_tensor_tensor(slot_e, ends[:, 0:NE].unsqueeze(1).to_broadcast([P, NB, NE]), float(P),
                                        bank_l[:, 0:NB * NE].rearrange("p (b e) -> p b e", e=NE), ALU.mult, ALU.add))
            settle()
            for k in range(2):
                do(dve.tensor_tensor(slot_m[:, k], mask[:, k], slot_e, ALU.mult))
            settle()
            with nc.allow_low_precision(reason="whole numbers below 4096"):
                do(dve.tensor_reduce(slot_u[:], slot_m.rearrange("p k b e -> p (k b) e"), AX.X, ALU.add))
            settle()
            do(dve.tensor_single_scalar(row_u[:], slot_u[:], P - 1, ALU.bitwise_and))
            do(dve.tensor_single_scalar(tile_u[:], slot_u[:], 7, ALU.logical_shift_right))
            settle()
            row_f_made = do(dve.tensor_copy(row_f[:], row_u[:]))
            dve.tensor_tensor(tile_hot, iota_t[:].unsqueeze(1).to_broadcast([P, 2 * NB, NTP]),
                              tile_u[:].unsqueeze(2).to_broadcast([P, 2 * NB, NTP]), ALU.is_equal).then_inc(tile_hot_ready, 1)
            need(row_f_made)
            for q in range(2 * NB):
                dve.tensor_scalar(row_hot[:, q, :], iota_r[:], row_f[:, q:q + 1], None,
                                  ALU.is_equal).then_inc(hot_ready, 1)
            dve.wait_ge(table_ready, 1)
            do(dve.scalar_tensor_tensor(pad_val[:], bank_l[:, 0:NTP], 0.0, pad_row[:], ALU.is_equal, ALU.mult))
            settle()
            dve.scalar_tensor_tensor(pair_u[:], bank_l[:, 0:NTP], -1.0, pad_val[:], ALU.add,
                                     ALU.add).then_inc(indices_ready, 1)
            dve.wait_ge(indices_ready, 1)
            dve.tensor_single_scalar(token_u[:], pair_u[:], NTOK - 1, ALU.bitwise_and).then_inc(indices_ready, 1)
            shared_h(NB - 2)
            shared_h(NB - 1)
            add_shared(NB - 3)
            do(dve.tensor_tensor(ended, ends[0:1, 1:NE + 1].unsqueeze(1).to_broadcast([1, NTP, NE]),
                                 iota_t[0:1, :].unsqueeze(2).to_broadcast([1, NTP, NE]), ALU.is_le))
            settle()
            do(dve.tensor_reduce(owner_f[:], ended, AX.X, ALU.add))
            settle()
            dve.tensor_scalar(owner[:], owner_f[:], float(NE - 1), None, ALU.min).then_inc(owner_ready, 1)
            def move_x(i, par):
                dve.wait_ge(xg_turned, i + 1)
                dve.tensor_copy(xgT[:, par].rearrange("p c t -> p (c t)"), t_bank[par][:, 0:DC * P]).then_inc(xgT_ready, 1)

            def gated(i, par):
                dve.wait_ge(sg_ready, i + 1)
                dve.tensor_tensor(h[:, par, :], sg[:, par, :], gu_bank[par][:, J:J2], ALU.mult).then_inc(h_ready, 1)

            def move_h(i, par):
                dve.wait_ge(h_turned, i + 1)
                dve.tensor_copy(hT[:, par].rearrange("p c t -> p (c t)"), ht_bank[par][0:JH, 0:2 * P]).then_inc(hT_ready, 1)

            def edge(i):
                if i + 2 < NT:
                    move_x(i + 2, i % 2)
                if 1 <= i <= NT:
                    move_h(i - 1, (i - 1) % 2)
                if i < NT:
                    gated(i, i % 2)

            move_x(0, 0)
            add_shared(NB - 2)
            add_shared(NB - 1)
            move_x(1, 1)
            edge(0)
            with dve.Fori(0, (NT - 3) // 2) as r:
                for u in range(2):
                    move_x(2 * r + (3 + u), 1 - u)
                    move_h(2 * r + u, u)
                    gated(2 * r + (1 + u), 1 - u)
            for i in range(NT - 2, NT + 1):
                edge(i)

            dve.tensor_tensor(esub, lg[:], top[:, :, 0:1].to_broadcast([P, NB, NE]),
                              ALU.subtract).then_inc(esub_ready, 1)
            dve.tensor_tensor(etop[:], top[:, :, 1], top[:, :, 0], ALU.subtract).then_inc(esub_ready, 1)
            dve.wait_ge(eexp_ready, 2)
            do(dve.tensor_reduce(esum[:], esub, AX.X, ALU.add))
            settle()
            do(dve.reciprocal(esum[:], esum[:]))
            settle()
            do(dve.tensor_scalar(wts[:, 0], esum[:], tg[:, 1:2], None, ALU.mult))
            settle()
            do(dve.tensor_tensor(wts[:, 1], wts[:, 0], etop[:], ALU.mult))
            settle()

            def first_choice(b):
                dve.wait_ge(y_back[b], 16)
                return do(dve.scalar_tensor_tensor(x1[:, b, :], y2[:, b, 0, :], wts[:, 0, b:b + 1], x1[:, b, :],
                                                   ALU.mult, ALU.add))

            def second_choice(b, n):
                if b == NB - 1:
                    dve.wait_ge(last_back, 16)
                need(n)
                dve.scalar_tensor_tensor(x1[:, b, :], y2[:, b, 1, :], wts[:, 1, b:b + 1], x1[:, b, :], ALU.mult,
                                         ALU.add).then_inc(out_ready, 1)

            ahead = first_choice(0)
            for b in range(1, NB):
                done, ahead = ahead, first_choice(b)
                second_choice(b - 1, done)
            second_choice(NB - 1, ahead)


_INS = ['x', 'ctx_2048', 'g_xattn', 'g_ffn', 'L0_xattn_time_decay', 'L0_xattn_time_first', 'L0_ffn_gate_w',
        'L0_ffn_w_gate_up', 'L0_ffn_w_down', 'L0_ffn_shared_gate_up', 'L0_ffn_shared_down']


def kernel(**inputs):
    import numpy as np
    import concourse.bacc as bacc
    from concourse.bass_utils import run_bass_kernel_spmd

    nc = bacc.Bacc("TRN2", target_bir_lowering=False, num_devices=1)
    arrays, args = {}, []
    for name in _INS:
        a = np.ascontiguousarray(inputs[name])
        arrays[f"in_{name}"] = a
        args.append(nc.dram_tensor(f"in_{name}", a.shape, mybir.dt.from_np(a.dtype), kind="ExternalInput").ap())
    out = nc.dram_tensor("out", inputs['x'].shape, F32, kind="ExternalOutput").ap()
    gated_wkv_moe(nc, *args, out)
    r = run_bass_kernel_spmd(nc, [arrays], core_ids=[0])
    return r.results[0]["out"]
```
